# Optimizing a Trainium2 kernel written in Bass

```python
import numpy as np
import jax
import jax.numpy as jnp

def _softmax(x, axis=-1):
    return jax.nn.softmax(x, axis=axis)
def _gelu(x):
    return jax.nn.gelu(x, approximate=True)
def _silu(x):
    return jax.nn.silu(x)
def _sigmoid(x):
    return jax.nn.sigmoid(x)
def _layernorm(x, axis=-1, eps=1e-5):
    m = jnp.mean(x, axis=axis, keepdims=True)
    v = jnp.var(x, axis=axis, keepdims=True)
    return (x - m) / jnp.sqrt(v + eps)
def _scatter_add(tgt, idx, src, axis=0):
    return tgt.at[idx].add(src)
def _segment_sum(src, seg, n):
    return jax.ops.segment_sum(src, seg, n)

kernel_name = 'mk_conv_preact_d2_conv_nchw32_b2f674'

def setup_inputs(seed: int = 0):
    np.random.seed(seed)
    _w = jnp.asarray
    def _rec_inputs():
        import jax
        import jax.numpy as jnp
        _gk = jax.random.key(seed)
        x = -0.000125 + 0.9999 * jax.random.normal(jax.random.fold_in(_gk, 1), (4, 32, 512, 512), jnp.float32)
        return x
    x = _rec_inputs()
    def _L0_conv_setup():
        import jax, jax.numpy as jnp
        import numpy as np
        from jax import lax
        key = jax.random.key(seed)
        k1, k2 = jax.random.split(key)
        X = jax.random.normal(k1, (4, 32, 512, 512), dtype=jnp.float32)
        kernel = jax.random.uniform(k2, (5, 5), dtype=jnp.float32)
        return {'X': X, 'kernel': kernel, 'stride': 1, 'padding': 2}
    _L0_conv_all = _L0_conv_setup()
    _L0_conv_in = {k: v for k, v in _L0_conv_all.items() if k in ('kernel', )}
    del _L0_conv_all

    def _L1_conv_setup():
        import jax, jax.numpy as jnp
        import numpy as np
        WS = 8
        S = 2
        GRID = jnp.linspace(-2.0, 2.0, 8)
        DENOM = 4.0 / 7.0

        def _layernorm(x, g, b, eps=1e-05):
            mu = x.mean(-1, keepdims=True)
            var = ((x - mu) ** 2).mean(-1, keepdims=True)
            return (x - mu) * jax.lax.rsqrt(var + eps) * g + b

        def _fastkan(x, ln_g, ln_b, ws, wb, bb):
            ln = _layernorm(x, ln_g, ln_b)
            basis = jnp.exp(-((ln[..., None] - GRID) / DENOM) ** 2)
            flat = basis.reshape(*basis.shape[:-2], -1)
            return flat @ ws.T + jax.nn.silu(x) @ wb.T + bb
        key = jax.random.key(seed)
        ks = jax.random.split(key, 16)
        d = {'x': jax.random.normal(ks[0], (4, 32, 256, 256), dtype=jnp.float32), 'pn_g': jnp.ones((32,), jnp.float32), 'pn_b': jnp.zeros((32,), jnp.float32), 'k1_ln_g': jnp.ones((16,), jnp.float32), 'k1_ln_b': jnp.zeros((16,), jnp.float32), 'k1_ws': jax.random.normal(ks[1], (16, 128), jnp.float32) * 0.1, 'k1_wb': jax.random.normal(ks[2], (16, 16), jnp.float32) * 0.1, 'k1_bb': jnp.zeros((16,), jnp.float32), 'k2_ln_g': jnp.ones((16,), jnp.float32), 'k2_ln_b': jnp.zeros((16,), jnp.float32), 'k2_ws': jax.random.normal(ks[3], (16, 128), jnp.float32) * 0.1, 'k2_wb': jax.random.normal(ks[4], (16, 16), jnp.float32) * 0.1, 'k2_bb': jnp.zeros((16,), jnp.float32), 'k3_ln_g': jnp.ones((32,), jnp.float32), 'k3_ln_b': jnp.zeros((32,), jnp.float32), 'k3_ws': jax.random.normal(ks[5], (32, 256), jnp.float32) * 0.1, 'k3_wb': jax.random.normal(ks[6], (32, 32), jnp.float32) * 0.1, 'k3_bb': jnp.zeros((32,), jnp.float32), 'k4_ln_g': jnp.ones((32,), jnp.float32), 'k4_ln_b': jnp.zeros((32,), jnp.float32), 'k4_ws': jax.random.normal(ks[7], (32, 256), jnp.float32) * 0.1, 'k4_wb': jax.random.normal(ks[8], (32, 32), jnp.float32) * 0.1, 'k4_bb': jnp.zeros((32,), jnp.float32)}
        return d
    _L1_conv_all = _L1_conv_setup()
    _L1_conv_in = {k: v for k, v in _L1_conv_all.items() if k in ('pn_g', 'pn_b', 'k1_ln_g', 'k1_ln_b', 'k1_ws', 'k1_wb', 'k1_bb', 'k2_ln_g', 'k2_ln_b', 'k2_ws', 'k2_wb', 'k2_bb', 'k3_ln_g', 'k3_ln_b', 'k3_ws', 'k3_wb', 'k3_bb', 'k4_ln_g', 'k4_ln_b', 'k4_ws', 'k4_wb', 'k4_bb', )}
    del _L1_conv_all

    return {
        "x": x,
        "L0_conv_kernel": _L0_conv_in["kernel"],
        "L1_conv_pn_g": _L1_conv_in["pn_g"],
        "L1_conv_pn_b": _L1_conv_in["pn_b"],
        "L1_conv_k1_ln_g": _L1_conv_in["k1_ln_g"],
        "L1_conv_k1_ln_b": _L1_conv_in["k1_ln_b"],
        "L1_conv_k1_ws": _L1_conv_in["k1_ws"],
        "L1_conv_k1_wb": _L1_conv_in["k1_wb"],
        "L1_conv_k1_bb": _L1_conv_in["k1_bb"],
        "L1_conv_k2_ln_g": _L1_conv_in["k2_ln_g"],
        "L1_conv_k2_ln_b": _L1_conv_in["k2_ln_b"],
        "L1_conv_k2_ws": _L1_conv_in["k2_ws"],
        "L1_conv_k2_wb": _L1_conv_in["k2_wb"],
        "L1_conv_k2_bb": _L1_conv_in["k2_bb"],
        "L1_conv_k3_ln_g": _L1_conv_in["k3_ln_g"],
        "L1_conv_k3_ln_b": _L1_conv_in["k3_ln_b"],
        "L1_conv_k3_ws": _L1_conv_in["k3_ws"],
        "L1_conv_k3_wb": _L1_conv_in["k3_wb"],
        "L1_conv_k3_bb": _L1_conv_in["k3_bb"],
        "L1_conv_k4_ln_g": _L1_conv_in["k4_ln_g"],
        "L1_conv_k4_ln_b": _L1_conv_in["k4_ln_b"],
        "L1_conv_k4_ws": _L1_conv_in["k4_ws"],
        "L1_conv_k4_wb": _L1_conv_in["k4_wb"],
        "L1_conv_k4_bb": _L1_conv_in["k4_bb"],
    }

def reference(x, L0_conv_kernel, L1_conv_pn_g, L1_conv_pn_b, L1_conv_k1_ln_g, L1_conv_k1_ln_b, L1_conv_k1_ws, L1_conv_k1_wb, L1_conv_k1_bb, L1_conv_k2_ln_g, L1_conv_k2_ln_b, L1_conv_k2_ws, L1_conv_k2_wb, L1_conv_k2_bb, L1_conv_k3_ln_g, L1_conv_k3_ln_b, L1_conv_k3_ws, L1_conv_k3_wb, L1_conv_k3_bb, L1_conv_k4_ln_g, L1_conv_k4_ln_b, L1_conv_k4_ws, L1_conv_k4_wb, L1_conv_k4_bb):
    import jax
    import jax.numpy as jnp
    def _L0_conv_ref(X, kernel, stride, padding):
        import jax, jax.numpy as jnp
        import numpy as np
        from jax import lax
        B, C, H, W = X.shape
        k = kernel.shape[0]
        Xf = X.reshape(B * C, 1, H, W)
        out = lax.conv_general_dilated(Xf, kernel[None, None, :, :], window_strides=(stride, stride), padding=[(padding, padding), (padding, padding)], dimension_numbers=('NCHW', 'OIHW', 'NCHW'))
        _, _, Ho, Wo = out.shape
        return out.reshape(B, C, Ho, Wo)

    def _L1_conv_ref(x, pn_g, pn_b, k1_ln_g, k1_ln_b, k1_ws, k1_wb, k1_bb, k2_ln_g, k2_ln_b, k2_ws, k2_wb, k2_bb, k3_ln_g, k3_ln_b, k3_ws, k3_wb, k3_bb, k4_ln_g, k4_ln_b, k4_ws, k4_wb, k4_bb):
        import jax, jax.numpy as jnp
        import numpy as np
        WS = 8
        S = 2
        GRID = jnp.linspace(-2.0, 2.0, 8)
        DENOM = 4.0 / 7.0

        def _layernorm(x, g, b, eps=1e-05):
            mu = x.mean(-1, keepdims=True)
            var = ((x - mu) ** 2).mean(-1, keepdims=True)
            return (x - mu) * jax.lax.rsqrt(var + eps) * g + b

        def _fastkan(x, ln_g, ln_b, ws, wb, bb):
            ln = _layernorm(x, ln_g, ln_b)
            basis = jnp.exp(-((ln[..., None] - GRID) / DENOM) ** 2)
            flat = basis.reshape(*basis.shape[:-2], -1)
            return flat @ ws.T + jax.nn.silu(x) @ wb.T + bb
        B, C, H, W = x.shape
        c = C // S
        xh = jnp.transpose(x, (0, 2, 3, 1))
        wins = xh.reshape(B, H // WS, WS, W // WS, WS, C).transpose(0, 1, 3, 2, 4, 5).reshape(-1, WS, WS, C)
        b = wins.shape[0]
        y = _layernorm(wins, pn_g, pn_b)
        a = y.reshape(b, WS, WS, c, S).transpose(0, 2, 3, 1, 4).reshape(b, WS * c, WS * S)
        a = _fastkan(a, k1_ln_g, k1_ln_b, k1_ws, k1_wb, k1_bb)
        a = a.reshape(b, WS, c, WS, S).transpose(0, 3, 1, 2, 4).reshape(b, WS, WS, C)
        d = y.reshape(b, WS, WS, c, S).transpose(0, 1, 3, 2, 4).reshape(b, WS * c, WS * S)
        d = _fastkan(d, k2_ln_g, k2_ln_b, k2_ws, k2_wb, k2_bb)
        d = d.reshape(b, WS, c, WS, S).transpose(0, 1, 3, 2, 4).reshape(b, WS, WS, C)
        e = _fastkan(y.reshape(b, WS * WS, C), k3_ln_g, k3_ln_b, k3_ws, k3_wb, k3_bb).reshape(b, WS, WS, C)
        z = a + d + e
        z = _fastkan(z.reshape(b, WS * WS, C), k4_ln_g, k4_ln_b, k4_ws, k4_wb, k4_bb).reshape(b, WS, WS, C)
        out = z + wins
        out = out.reshape(B, H // WS, W // WS, WS, WS, C).transpose(0, 1, 3, 2, 4, 5).reshape(B, H, W, C)
        return jnp.transpose(out, (0, 3, 1, 2))

    def _gn(v, G=16, eps=1e-5):
        B_, C_, H_, W_ = v.shape
        g = v.reshape(B_, G, C_ // G, H_, W_)
        m = jnp.mean(g, axis=(2, 3, 4), keepdims=True)
        s = jnp.var(g, axis=(2, 3, 4), keepdims=True)
        return ((g - m) / jnp.sqrt(s + eps)).reshape(v.shape)

    def _ln_c(v, eps=1e-6):
        m = jnp.mean(v, axis=1, keepdims=True)
        s = jnp.var(v, axis=1, keepdims=True)
        return (v - m) / jnp.sqrt(s + eps)

    def _ln_t(v, eps=1e-5):
        m = jnp.mean(v, axis=-1, keepdims=True)
        s = jnp.var(v, axis=-1, keepdims=True)
        return (v - m) / jnp.sqrt(s + eps)

    def _to_tokens(v):
        B_, C_, H_, W_ = v.shape
        return v.reshape(B_, C_, H_ * W_).transpose(0, 2, 1)
    def _from_tokens(t, like):
        B_, C_, H_, W_ = like.shape
        return t.transpose(0, 2, 1).reshape(B_, C_, H_, W_)

    x = x + _L0_conv_ref(_gn(x), L0_conv_kernel, 1, 2)
    x = x + _L1_conv_ref(_gn(x), L1_conv_pn_g, L1_conv_pn_b, L1_conv_k1_ln_g, L1_conv_k1_ln_b, L1_conv_k1_ws, L1_conv_k1_wb, L1_conv_k1_bb, L1_conv_k2_ln_g, L1_conv_k2_ln_b, L1_conv_k2_ws, L1_conv_k2_wb, L1_conv_k2_bb, L1_conv_k3_ln_g, L1_conv_k3_ln_b, L1_conv_k3_ws, L1_conv_k3_wb, L1_conv_k3_bb, L1_conv_k4_ln_g, L1_conv_k4_ln_b, L1_conv_k4_ws, L1_conv_k4_wb, L1_conv_k4_bb)
    return x


_drawn_inputs = setup_inputs


def setup_inputs(seed=0):
    import zlib

    import numpy as np

    out = dict(_drawn_inputs(seed))
    spreads = {'L1_conv_pn_g': (1.0, 0.2),
     'L1_conv_pn_b': (0.0, 0.1),
     'L1_conv_k1_ln_g': (1.0, 0.549),
     'L1_conv_k1_ln_b': (0.0, 0.38),
     'L1_conv_k1_bb': (0.0, 0.368),
     'L1_conv_k2_ln_g': (1.0, 0.557),
     'L1_conv_k2_ln_b': (0.0, 0.357),
     'L1_conv_k2_bb': (0.0, 0.347),
     'L1_conv_k3_ln_g': (1.0, 0.2),
     'L1_conv_k3_ln_b': (0.0, 0.1),
     'L1_conv_k3_bb': (0.0, 0.1),
     'L1_conv_k4_ln_g': (1.0, 0.2),
     'L1_conv_k4_ln_b': (0.0, 0.315),
     'L1_conv_k4_bb': (0.0, 0.291)}
    factors = {}
    for name, (base, spread) in spreads.items():
        noise = np.random.default_rng([zlib.crc32(name.encode()), seed]).standard_normal(out[name].shape)
        drawn = base * np.exp(spread * noise) if base else spread * noise
        out[name] = jnp.asarray(drawn.astype(out[name].dtype))
    for name, factor in factors.items():
        out[name] = (out[name] * factor).astype(out[name].dtype)
    return out
```

```python
import concourse.bass as bass
from concourse import mybir
from contextlib import ExitStack
import numpy as np

F32 = mybir.dt.float32
I32 = mybir.dt.int32
ALU = mybir.AluOpType
ACT = mybir.ActivationFunctionType
AX = mybir.AxisListType

P = 128
C = 32
CP = C // 2
WS = 8
NB = 8
BR = 104
FREE = WS * WS * C
QT = FREE // 4
RSQRT_GUESS = 1597463007.0

LAYERS = ("a", "d", "e", "z")
W_COLS = 192
BIAS_COL = 4 * W_COLS
M2_COL = BIAS_COL + 4
N_COLS = M2_COL + 3
ROWS = {}
_at = 0
for _n, _k in (("gp", C), ("bp", C), ("ge", C), ("be", C), ("gz", C), ("bz", C), ("gd", 16), ("bd", 16),
               ("ga", 16), ("ba", 16), ("kern", 25)):
    ROWS[_n] = (_at, _k)
    _at += _k
N_ROWS = _at


def view(tile, offset, dims, parts=P, first=0):
    step = tile[:, :].ap[0][0]
    return bass.AP(tensor=tile[:, :].tensor, offset=first * step + offset, ap=[[step, parts]] + [list(d) for d in dims])


def conv_kan_kernel(nc, x, cols, rows, ident_in, shift_in, ones_in, mask_in, out):
    B, _, H, W = x.shape
    NG = B * CP
    NBLK = -(-H // BR)
    LAST = H - BR * (NBLK - 1)
    XW = W + 4
    NT = B * H // 16
    TB = H // 16
    CHUNKS = 2 * NBLK
    KR = BR + 4
    assert W == 512 and H % 16 == 0 and LAST % 8 == 0

    y0 = nc.dram_tensor("y0", [B, 2, CP, H, W], F32).ap()
    gn2 = nc.dram_tensor("gn2", [B, CP, 3], F32).ap()
    xg = x.rearrange("b (c s) h w -> (b c) s h w", s=2)

    ctx = ExitStack()
    with ctx:
        def sem(name):
            return ctx.enter_context(nc.semaphore(name))

        with ExitStack() as c1:
            def sb(name, shape, dt=F32):
                return c1.enter_context(nc.sbuf_tensor(name, shape, dt))

            def pb(name, n=512):
                return c1.enter_context(nc.psum_tensor(name, [P, n], F32))

            X = [sb(f"X{k}", [P, 2, NBLK, XW]) for k in range(2)]
            Y = [sb(f"Y{k}", [P, 2, NBLK, W]) for k in range(2)]
            ones = sb("ones", [P, NBLK, XW])
            shifts = sb("shifts", [P, 5, BR])
            band = sb("band", [P, 5, BR])
            gband = [sb(f"gband{k}", [P, 5, BR]) for k in range(2)]
            smap = sb("smap", [P, NBLK, W])
            kern = sb("kern", [P, 25])
            mask = sb("mask", [P, P])
            allrows = sb("allrows", [P, P])
            bs = sb("bs", [P, CHUNKS, 6])
            bsq = sb("bsq", [P, CHUNKS, 2])
            ysq = sb("ysq", [P, CHUNKS, 2])
            ys = sb("ys", [P, CHUNKS, 6])
            part1 = sb("part1", [P, 2])
            part2 = sb("part2", [P, 2 * NG])
            st = sb("st", [P, 2])
            nw = sb("nw", [P, 4])
            nrm = [sb(f"nrm{k}", [P, 1]) for k in range(2)]
            g2 = sb("g2", [P, 2 * NG])
            g2w = sb("g2w", [P, 4 * NG])
            g2o = sb("g2o", [P, NG, 3])
            pc = [pb(f"pc{k}") for k in range(NBLK)]
            pst = pb("pst")
            p2 = pb("p2")

            const_loaded = sem("const_loaded")
            cleared = sem("cleared")
            x_loaded = [sem(f"x_loaded{k}") for k in range(2)]
            y_stored = [sem(f"y_stored{k}") for k in range(2)]
            band_ready = sem("band_ready")
            part1_ready = sem("part1_ready")
            sums1_ready = sem("sums1_ready")
            gband_ready = sem("gband_ready")
            chunk_ready = sem("chunk_ready")
            chunk_used = sem("chunk_used")
            conv_done = sem("conv_done")
            y_ready = sem("y_ready")
            v1 = sem("v1")
            sums2_ready = sem("sums2_ready")
            gn2_ready = sem("gn2_ready")
            gn2_stored = sem("gn2_stored")

            block = c1.enter_context(nc.Block())
            LOADS = NBLK + 1

            @block.sync
            def _(sp):
                for dst, src in ((shifts[:, :, :], shift_in), (ones[:, :, :], ones_in), (mask[:, :], mask_in)):
                    sp.dma_start(dst, src).then_inc(const_loaded, 16)
                at, n = ROWS["kern"]
                sp.dma_start(kern[:, :], rows[:, at:at + n].partition_broadcast(P)).then_inc(const_loaded, 16)
                sp.wait_ge(cleared, 2)

                def load(k, n):
                    xn = xg[n].rearrange("s h w -> h s w")
                    sp.dma_start(X[k][2:BR + 2, :, 0, 2:W + 2], xn[0:BR]).then_inc(x_loaded[k], 16)
                    sp.dma_start(X[k][BR + 2:KR, :, 0, 2:W + 2], xn[BR:BR + 2]).then_inc(x_loaded[k], 16)
                    for b in range(1, NBLK):
                        r = KR if b < NBLK - 1 else LAST + 2
                        sp.dma_start(X[k][0:r, :, b, 2:W + 2], xn[BR * b - 2:BR * b - 2 + r]).then_inc(x_loaded[k], 16)

                load(0, 0)
                load(1, 1)
                with sp.Fori(1, NG // 2) as m:
                    for k in range(2):
                        sp.wait_ge(conv_done, 2 * m + k - 1)
                        load(k, 2 * m + k)
                sp.wait_ge(gn2_ready, 1)
                sp.dma_start(gn2.rearrange("(o b) c k -> o (b c) k", o=1), g2o[0:1, :, :]).then_inc(gn2_stored, 16)
                sp.wait_ge(gn2_stored, 16)

            @block.gpsimd
            def _(pool):
                for k in range(2):
                    nc.gpsimd.memset(X[k][:, :, :, :], 0.0).then_inc(cleared, 1)

            @block.scalar
            def _(act):
                def store(k, n):
                    yn = y0[n // CP, :, n % CP].rearrange("s h w -> h s w")
                    for b in range(NBLK):
                        r = BR if b < NBLK - 1 else LAST
                        act.dma_start(yn[BR * b:BR * b + r], Y[k][0:r, :, b, :]).then_inc(y_stored[k], 16)

                with act.Fori(0, NG // 2) as m:
                    for k in range(2):
                        act.wait_ge(y_ready, 2 * m + k + 1)
                        store(k, 2 * m + k)
                for k in range(2):
                    act.wait_ge(y_stored[k], 16 * NBLK * (NG // 2))

            @block.vector
            def _(dve):
                steps = {"base": 0, "n": 0}

                def step(ins):
                    steps["n"] += 1
                    return ins.then_inc(v1, 1)

                def settle():
                    dve.wait_ge(v1, steps["base"] + steps["n"])

                def rsqrt(y, v, h, t):
                    step(nc.vector.tensor_scalar(y.bitcast(I32), v.bitcast(I32), -0.5, RSQRT_GUESS, ALU.mult, ALU.add))
                    step(nc.vector.tensor_scalar(h, v, -0.5, None, ALU.mult))
                    for _ in range(3):
                        settle()
                        step(nc.vector.tensor_tensor(t, y, y, ALU.mult))
                        settle()
                        step(nc.vector.tensor_tensor(t, t, h, ALU.mult))
                        settle()
                        step(nc.vector.scalar_tensor_tensor(out=y, in0=t, scalar=1.5, in1=y, op0=ALU.add, op1=ALU.mult))
                    settle()

                def mean_parts(stats, sq, dst0, dst1, parts):
                    n = CHUNKS
                    means = view2(stats, 1, [[6, n], [3, 2]], parts)
                    m2 = view2(stats, 2, [[6, n], [3, 2]], parts)
                    step(nc.vector.tensor_tensor(sq[0:parts, :, :], means, means, ALU.mult))
                    settle()
                    step(nc.vector.scalar_tensor_tensor(out=sq[0:parts, :, :], in0=m2, scalar=1.0 / 256, in1=sq[0:parts, :, :],
                                                        op0=ALU.mult, op1=ALU.add))
                    settle()
                    step(nc.vector.tensor_reduce(dst0, means, AX.XY, ALU.add))
                    return nc.vector.tensor_reduce(dst1, sq[0:parts, :, :], AX.XY, ALU.add)

                def view2(tile, offset, dims, parts):
                    stp = tile[:, :, :].ap[0][0]
                    return bass.AP(tensor=tile[:, :, :].tensor, offset=offset, ap=[[stp, parts]] + dims)

                step(nc.vector.memset(allrows[:, :], 1.0 / (4 * H)))
                step(nc.vector.memset(part2[:, :], 0.0))
                step(nc.vector.memset(ys[:, :, :], 0.0))
                step(nc.vector.memset(smap[:, :, :], 0.0))
                dve.wait_ge(const_loaded, 64)
                for dy in range(5):
                    for dx in range(5):
                        w = kern[:, 5 * dy + dx:5 * dy + dx + 1]
                        if dy == 0:
                            ins = nc.vector.tensor_scalar(band[:, dx, :], shifts[:, dy, :], w, None, ALU.mult)
                        else:
                            ins = nc.vector.scalar_tensor_tensor(out=band[:, dx, :], in0=shifts[:, dy, :], scalar=w,
                                                                 in1=band[:, dx, :], op0=ALU.mult, op1=ALU.add)
                        step(ins)
                    settle()
                nc.vector.tensor_copy(kern[:, 0:1], kern[:, 0:1]).then_inc(band_ready, 1)
                for b in range(NBLK):
                    r = BR if b < NBLK - 1 else LAST
                    dve.wait_ge(chunk_ready, b + 1)
                    nc.vector.tensor_copy(smap[0:r, b, :], pc[b][0:r, :]).then_inc(chunk_used, 1)

                def sums(k, n, loads):
                    dve.wait_ge(x_loaded[k], loads)
                    for i in range(CHUNKS):
                        step(nc.vector.bn_stats(bs[0:KR, i, :], X[k][0:KR, i // NBLK, i % NBLK, 2:W + 2]))
                    settle()
                    mean_parts(bs, bsq, part1[0:KR, 0:1], part1[0:KR, 1:2], KR).then_inc(part1_ready, 1)

                def norm(k, n):
                    dve.wait_ge(sums1_ready, n + 1)
                    step(nc.vector.tensor_copy(st[:, :], pst[:, 0:2]))
                    settle()
                    step(nc.vector.tensor_tensor(nw[:, 0:1], st[:, 0:1], st[:, 0:1], ALU.mult))
                    settle()
                    step(nc.vector.tensor_tensor(nw[:, 0:1], st[:, 1:2], nw[:, 0:1], ALU.subtract))
                    settle()
                    step(nc.vector.tensor_scalar(nw[:, 0:1], nw[:, 0:1], 0.0, 1e-5, ALU.max, ALU.add))
                    settle()
                    rsqrt(nw[:, 1:2], nw[:, 0:1], nw[:, 2:3], nw[:, 3:4])
                    step(nc.vector.scalar_tensor_tensor(out=nrm[k][:, :], in0=st[:, 0:1], scalar=-1.0, in1=nw[:, 1:2],
                                                        op0=ALU.mult, op1=ALU.mult))
                    step(nc.vector.tensor_scalar(gband[k][:, :, :], band[:, :, :], nw[:, 1:2], None, ALU.mult))
                    settle()
                    nc.vector.tensor_tensor(gband[k][:, 2, :], gband[k][:, 2, :], shifts[:, 2, :],
                                            ALU.add).then_inc(gband_ready, 1)

                def evacuate(k, n, i0, i1, stored):
                    if stored is not None:
                        dve.wait_ge(y_stored[k], stored)
                    for i in range(i0, i1):
                        s, b = divmod(i, NBLK)
                        r = BR if b < NBLK - 1 else LAST
                        dve.wait_ge(chunk_ready, NBLK + CHUNKS * n + i + 1)
                        nc.vector.scalar_tensor_tensor(out=Y[k][0:r, s, b, :], in0=smap[0:r, b, :], scalar=nrm[k][0:r, 0:1],
                                                       in1=pc[i % NBLK][0:r, :], op0=ALU.mult,
                                                       op1=ALU.add).then_inc(chunk_used, 1)
                    dve.wait_ge(chunk_used, NBLK + CHUNKS * n + i1)
                    for i in range(i0, i1):
                        s, b = divmod(i, NBLK)
                        r = BR if b < NBLK - 1 else LAST
                        ins = step(nc.vector.bn_stats(ys[0:r, i, :], Y[k][0:r, s, b, :]))

                def group(k, n, stored, nxt):
                    if nxt is not None:
                        sums(1 - k, n + 1, nxt)
                    evacuate(k, n, 0, NBLK, stored)
                    if nxt is not None:
                        norm(1 - k, n + 1)
                    evacuate(k, n, NBLK, CHUNKS, None)
                    settle()
                    ins = mean_parts(ys, ysq, part2[0:BR, bass.ds(2 * n, 1)], part2[0:BR, bass.ds(2 * n + 1, 1)], BR)
                    ins.then_inc(y_ready, 1)

                PER_LOAD = 16 * LOADS
                PER_STORE = 16 * NBLK
                sums(0, 0, PER_LOAD)
                norm(0, 0)
                group(0, 0, None, PER_LOAD)
                group(1, 1, None, 2 * PER_LOAD)
                head = steps["n"]
                with dve.Fori(1, NG // 2 - 1) as m:
                    steps["n"] = 0
                    per = steps.get("per", 0)
                    steps["base"] = head + (m - 1) * GROUP_PAIR_STEPS(CHUNKS)
                    group(0, 2 * m, PER_STORE * m, PER_LOAD * (m + 1))
                    group(1, 2 * m + 1, PER_STORE * m, PER_LOAD * (m + 2))
                    assert steps["n"] == GROUP_PAIR_STEPS(CHUNKS), steps["n"]
                steps["base"] = head + (NG // 2 - 2) * GROUP_PAIR_STEPS(CHUNKS)
                steps["n"] = 0
                m = NG // 2 - 1
                group(0, 2 * m, PER_STORE * m, PER_LOAD * (m + 1))
                group(1, 2 * m + 1, PER_STORE * m, None)
                dve.wait_ge(sums2_ready, 1)
                step(nc.vector.tensor_copy(g2[:, :], p2[:, 0:2 * NG]))
                settle()
                mean, square = g2[:, 0:2 * NG:2], g2[:, 1:2 * NG:2]
                var, y, h, t = (g2w[:, q * NG:(q + 1) * NG] for q in range(4))
                step(nc.vector.tensor_tensor(var, mean, mean, ALU.mult))
                settle()
                step(nc.vector.tensor_tensor(var, square, var, ALU.subtract))
                settle()
                step(nc.vector.tensor_scalar(var, var, 0.0, 1e-5, ALU.max, ALU.add))
                settle()
                rsqrt(y, var, h, t)
                step(nc.vector.tensor_copy(g2o[:, :, 0], y))
                step(nc.vector.tensor_scalar(g2o[:, :, 2], y, 1.0, None, ALU.add))
                step(nc.vector.scalar_tensor_tensor(out=g2o[:, :, 1], in0=mean, scalar=-1.0, in1=y, op0=ALU.mult,
                                                    op1=ALU.mult))
                settle()
                nc.vector.tensor_copy(g2o[:, :, 0], y).then_inc(gn2_ready, 1)

            @block.tensor
            def _(pe):
                def conv(weights, src, bank, r):
                    for dx in range(5):
                        last = nc.tensor.matmul(pc[bank][0:BR, :], weights[0:KR, dx, :], src[0:KR, dx:dx + W],
                                                start=(dx == 0), stop=(dx == 4))
                    return last.then_inc(chunk_ready, 1)

                def sums1():
                    nc.tensor.matmul(pst[:, 0:2], mask[0:KR, :], part1[0:KR, :], start=True,
                                     stop=True).then_inc(sums1_ready, 1)

                pe.wait_ge(band_ready, 1)
                for b in range(NBLK):
                    conv(band, ones[:, b, :], b, BR)
                pe.wait_ge(part1_ready, 1)
                sums1()

                def group(k, n, more):
                    pe.wait_ge(gband_ready, n + 1)
                    for i in range(CHUNKS):
                        pe.wait_ge(chunk_used, CHUNKS * n + i + 1)
                        last = conv(gband[k], X[k][:, i // NBLK, i % NBLK, :], i % NBLK, BR)
                        if i == NBLK - 1 and more:
                            pe.wait_ge(part1_ready, n + 2)
                            sums1()
                    nc.tensor.matmul(p2[0:1, 0:1], mask[0:1, 0:1], mask[0:1, 0:1], start=True, stop=True).then_inc(conv_done, 1)

                with pe.Fori(0, NG // 2 - 1) as m:
                    group(0, 2 * m, True)
                    group(1, 2 * m + 1, True)
                group(0, NG - 2, True)
                group(1, NG - 1, False)
                pe.wait_ge(y_ready, NG)
                nc.tensor.matmul(p2[:, 0:2 * NG], allrows[0:BR, :], part2[0:BR, :], start=True,
                                 stop=True).then_inc(sums2_ready, 1)

        phase2(nc, ctx, y0, gn2, cols, rows, ident_in, out, B, H, W, NT, TB)


def GROUP_PAIR_STEPS(chunks):
    return 2 * (chunks + 3 + 4 + 11 + 2 + chunks + 3)


def phase2(nc, ctx, y0, gn2, cols, rows, ident_in, out, B, H, W, NT, TB):
    def sb(name, shape, dt=F32):
        return ctx.enter_context(nc.sbuf_tensor(name, shape, dt))

    def sem(name):
        return ctx.enter_context(nc.semaphore(name))

    wcols = sb("wcols", [P, N_COLS])
    wrows = sb("wrows", [P, N_ROWS])
    ident = sb("ident", [P, P])
    la = sb("la", [P, 4 * W])
    lscal = sb("lscal", [P, 2])
    res = sb("res", [P, 4 * W])
    rscal = sb("rscal", [P, 2])
    rbias = sb("rbias", [P, 1])
    yt = sb("yt", [P, FREE])
    va = sb("va", [P, FREE])
    vd = sb("vd", [P, FREE])
    ve = sb("ve", [P, FREE])
    vx = sb("vx", [P, FREE])
    sy = sb("sy", [P, FREE])
    sya = sb("sya", [P, FREE])
    syd = sb("syd", [P, FREE])
    zt = sb("zt", [P, FREE])
    sz = sb("sz", [P, FREE])
    sq = [sb(f"sq{k}", [P, FREE]) for k in range(2)]
    ex = [sb(f"ex{k}", [P, NB * QT]) for k in range(2)]
    basis = [sb(f"basis{k}", [P, 4 * 2 * 512]) for k in range(2)]
    silt = [sb(f"silt{k}", [P, 512]) for k in range(2)]
    usb = [sb(f"usb{k}", [P, 512]) for k in range(2)]
    mu = sb("mu", [P, 1088])
    var = sb("var", [P, 320])
    rs = sb("rs", [P, 640])
    nwh = sb("nwh", [P, 320])
    nwt = sb("nwt", [P, 320])
    flag = sb("flag", [P, 2])

    ps_sil = ctx.enter_context(nc.psum_tensor("ps_sil", [P, 512], F32))
    ps_back = ctx.enter_context(nc.psum_tensor("ps_back", [P, 512], F32))
    ps_ex = ctx.enter_context(nc.psum_tensor("ps_ex", [P, 2, 1024], F32))
    ps_u = [ctx.enter_context(nc.psum_tensor(f"ps_u{k}", [P, 512], F32)) for k in range(2)]

    w_loaded = sem("w_loaded")
    w_ready = sem("w_ready")
    l_loaded = sem("l_loaded")
    la_ready = sem("la_ready")
    int_ready = sem("int_ready")
    xn_ready = sem("xn_ready")
    cp_ready = sem("cp_ready")
    ca_ready = sem("ca_ready")
    cd_ready = sem("cd_ready")
    ce_ready = sem("ce_ready")
    cz_ready = sem("cz_ready")
    sqp_ready = sem("sqp_ready")
    sqa_ready = sem("sqa_ready")
    sqd_ready = sem("sqd_ready")
    sqe_ready = sem("sqe_ready")
    sqz_ready = sem("sqz_ready")
    y_norm = sem("y_norm")
    tanh_y = sem("tanh_y")
    sy_ready = sem("sy_ready")
    syo_ready = sem("syo_ready")
    z_ready = sem("z_ready")
    tanh_z = sem("tanh_z")
    sz_ready = sem("sz_ready")
    r_loaded = sem("r_loaded")
    rbias_ready = sem("rbias_ready")
    res_ready = sem("res_ready")
    ex_ready = sem("ex_ready")
    ext_ready = sem("ext_ready")
    basis_ready = sem("basis_ready")
    sil_ready = sem("sil_ready")
    silt_ready = sem("silt_ready")
    u_ready = sem("u_ready")
    usb_ready = sem("usb_ready")
    back_ready = sem("back_ready")
    back_used = sem("back_used")
    o_ready = sem("o_ready")
    o_stored = sem("o_stored")
    v2 = sem("v2")

    WIDX = {name: n for n, name in enumerate(LAYERS)}
    SRC = {"a": vx, "d": va, "e": vd, "z": ve}
    SILU = {"a": sya, "d": syd, "e": sy, "z": sz}

    def w_half(name, h):
        at = WIDX[name] * W_COLS + 32 * h
        return wcols[:, at:at + 32]

    def w_base(name):
        at = WIDX[name] * W_COLS + 64
        return wcols[:, at:at + 128]

    def bias_col(name):
        at = BIAS_COL + WIDX[name]
        return wcols[:, at:at + 1]

    def quarters(t, tail=False):
        first = isinstance(t, int) and t == 0
        names = "z" if tail else "ade" if first else "zade"
        return [(name, q) for name in names for q in range(4)]

    def base(t):
        if isinstance(t, int) and t == 0:
            return 0, 0, 0
        return 16 * t - 4, 12 * t, 4 * t - 4

    def counts(t, items, p):
        n0, m0, z0 = base(t)
        m = sum(name != "z" for name, _ in items[:p])
        return n0 + p, m0 + m, z0 + p - m

    def back_bank(items, p):
        return ps_sil if p == len(items) - 1 else ps_back

    def wait(eng, s, value):
        if isinstance(value, int) and value <= 0:
            return
        eng.wait_ge(s, value)

    def iterations(eng, body, tail):
        body(0)
        with eng.Fori(1, NT) as t:
            body(t)
        tail(NT)

    block = ctx.enter_context(nc.Block())

    @block.sync
    def _(sp):
        sp.dma_start(wcols[:, :], cols).then_inc(w_loaded, 16)
        sp.dma_start(wrows[:, :], rows.partition_broadcast(P)).then_inc(w_loaded, 16)
        sp.dma_start(ident[:, :], ident_in).then_inc(w_loaded, 16)

        def load_windows(t):
            b, r0 = t // TB, (t % TB) * 16
            wait(sp, int_ready, 2 * t)
            for s in range(2):
                for wr in range(2):
                    src = y0[b, s, :, bass.ds(r0 + 8 * wr, 8), :]
                    at = 1024 * s + 512 * wr
                    sp.dma_start(la[:, at:at + 512], src).then_inc(l_loaded, 16)
            sp.dma_start(lscal[:, :], gn2[b, :, 0:2].unsqueeze(1).to_broadcast([CP, WS, 2])).then_inc(l_loaded, 16)

        def load_result(t):
            b, r0 = t // TB, (t % TB) * 16
            for g in range(4):
                for s in range(2):
                    src = y0[b, s, :, bass.ds(r0, 16), :].rearrange("c (wr g i) w -> g c wr (i w)", wr=2, i=2)[g]
                    p0 = 32 * g + 16 * s
                    sp.dma_start(res[p0:p0 + 16, :].rearrange("p (r w) -> p r w", r=2), src).then_inc(r_loaded, 16)
                    sp.dma_start(rscal[p0:p0 + 16, :], gn2[b, :, 1:3]).then_inc(r_loaded, 16)

        def store_result(t):
            b, r0 = t // TB, (t % TB) * 16
            sp.wait_ge(o_ready, 4 * t + 4)
            ov = out[b].rearrange("(c s) h w -> s c h w", s=2)
            for g in range(4):
                for s in range(2):
                    dst = ov[s, :, bass.ds(r0, 16), :].rearrange("c (wr g i) w -> g c wr (i w)", wr=2, i=2)[g]
                    p0 = 32 * g + 16 * s
                    sp.dma_start(dst, res[p0:p0 + 16, :].rearrange("p (r w) -> p r w", r=2)).then_inc(o_stored, 16)

        def body(t):
            load_windows(t)
            if not (isinstance(t, int) and t == 0):
                store_result(t - 1)
                sp.wait_ge(o_stored, 128 * t)
            load_result(t)

        iterations(sp, body, lambda t: store_result(t - 1))
        sp.wait_ge(o_stored, 128 * NT)

    @block.scalar
    def _(act):
        def body(t, tail=False):
            first = isinstance(t, int) and t == 0
            if not tail:
                act.wait_ge(l_loaded, 80 * (t + 1))
                nc.scalar.activation(la[:, :], la[:, :], ACT.Identity, scale=lscal[:, 0:1],
                                     bias=lscal[:, 1:2]).then_inc(la_ready, 1)
                wait(act, ex_ready, 16 * t - 15)
                for k in range(2):
                    act.wait_ge(int_ready, 2 * t + k + 1)
                    nc.scalar.activation(view(yt, 128 * k, [[1, 128], [256, 8]]),
                                         ps_ex[:, k, :].rearrange("p (f i) -> p f i", i=8),
                                         ACT.Copy).then_inc(xn_ready, 1)
                act.wait_ge(cp_ready, t + 1)
                nc.scalar.activation(sq[0][:, :], yt[:, :], ACT.Square).then_inc(sqp_ready, 1)
                act.wait_ge(y_norm, t + 1)
                nc.scalar.activation(sq[1][:, :], yt[:, :], ACT.Tanh, scale=0.5).then_inc(tanh_y, 1)
                act.wait_ge(ca_ready, t + 1)
                nc.scalar.activation(sq[0][:, :], va[:, :], ACT.Square).then_inc(sqa_ready, 1)
                act.wait_ge(sy_ready, t + 1)
                act.wait_ge(cd_ready, t + 1)
                nc.scalar.activation(sq[1][:, :], vd[:, :], ACT.Square).then_inc(sqd_ready, 1)
                wait(act, sil_ready, base(t)[0])
                for s in range(2):
                    nc.scalar.activation(view(sya, s, [[2, 8], [256, 8], [16, 16]]),
                                         view(sy, 16 * s, [[256, 8], [32, 8], [1, 16]]), ACT.Copy).then_inc(syo_ready, 1)
                nc.scalar.activation(view(syd, 0, [[256, 8], [1, 16], [16, 16]]),
                                     view(sy, 0, [[256, 8], [16, 16], [1, 16]]), ACT.Copy).then_inc(syo_ready, 1)
                act.wait_ge(ce_ready, t + 1)
                nc.scalar.activation(sq[0][:, :], ve[:, :], ACT.Square).then_inc(sqe_ready, 1)
            if not first:
                act.wait_ge(rbias_ready, t)
                nc.scalar.activation(res[:, :], res[:, :], ACT.Identity, scale=rscal[:, 1:2],
                                     bias=rbias[:, 0:1]).then_inc(res_ready, 1)
                act.wait_ge(z_ready, t)
                nc.scalar.activation(sq[1][:, :], zt[:, :], ACT.Tanh, scale=0.5).then_inc(tanh_z, 1)
                act.wait_ge(cz_ready, t)
                nc.scalar.activation(sq[0][:, :], yt[:, :], ACT.Square).then_inc(sqz_ready, 1)
            items = quarters(t, tail)

            def evacuate(p):
                n, m, _ = counts(t, items, p)
                name, q = items[p]
                if name == "z":
                    return
                act.wait_ge(u_ready, n + 1)
                wait(act, back_ready, m - 1)
                nc.scalar.activation(usb[q % 2][:, :], ps_u[q % 2][:, :], ACT.Identity,
                                     bias=bias_col(name)).then_inc(usb_ready, 1)

            for p, (name, q) in enumerate(items):
                n, m, _ = counts(t, items, p)
                act.wait_ge(sil_ready, n + 1)
                wait(act, u_ready, n - 1)
                nc.scalar.activation(silt[q % 2][:, :], ps_sil[:, :], ACT.Copy).then_inc(silt_ready, 1)
                for g in range(4):
                    act.wait_ge(ext_ready, 4 * n + g + 1)
                    nc.scalar.activation(basis[q % 2][:, 1024 * g:1024 * g + 1024], ps_ex[:, g % 2, :], ACT.Exp,
                                         scale=-1.0).then_inc(basis_ready, 1)
                if p >= 1:
                    evacuate(p - 1)
            evacuate(len(items) - 1)

        act.wait_ge(w_ready, 1)
        iterations(act, body, lambda t: body(t, True))

    @block.vector
    def _(dve):
        steps = {"base": 0, "n": 0}

        def step(ins):
            steps["n"] += 1
            return ins.then_inc(v2, 1)

        def settle():
            dve.wait_ge(v2, steps["base"] + steps["n"])

        TT, TS, STT = nc.vector.tensor_tensor, nc.vector.tensor_scalar, nc.vector.scalar_tensor_tensor

        def rsqrt(n, v):
            y, h, t = rs[:, 0:n], nwh[:, 0:n], nwt[:, 0:n]
            step(TS(y.bitcast(I32), v.bitcast(I32), -0.5, RSQRT_GUESS, ALU.mult, ALU.add))
            step(TS(h, v, -0.5, None, ALU.mult))
            for _ in range(3):
                settle()
                step(TT(t, y, y, ALU.mult))
                settle()
                step(TT(t, t, h, ALU.mult))
                settle()
                step(STT(out=y, in0=t, scalar=1.5, in1=y, op0=ALU.add, op1=ALU.mult))
            settle()

        dve.wait_ge(w_loaded, 48)
        at, end = ROWS["ge"][0], ROWS["kern"][0]
        step(TS(wrows[:, at:end], wrows[:, at:end], 1.75, None, ALU.mult))
        for name in LAYERS:
            step(TS(w_base(name), w_base(name), 0.5, None, ALU.mult))
            for h in range(2):
                col = M2_COL + (0 if name in "ad" else 1 + h)
                step(TS(w_half(name, h), w_half(name, h), wcols[:, col:col + 1], None, ALU.mult))
        settle()
        nc.vector.memset(flag[:, :], 0.0).then_inc(w_ready, 1)

        ALL = {"e": [[32, 64], [1, 32]], "d": [[256, 8], [16, 16], [1, 16]], "a": [[256, 8], [1, 256]]}
        STAT = {"e": [[1, 64], [0, 32]], "d": [[16, 8], [0, 16], [1, 16]], "a": [[0, 8], [1, 256]]}
        HALF = [[32, 8], [1, 16]]

        def sums(tile, at, src, kind):
            if kind == "e":
                ins = nc.vector.tensor_reduce(view(tile, at, [[1, 64]]), view(src, 0, [[32, 64], [1, 32]]), AX.X, ALU.add)
            elif kind == "d":
                ins = nc.vector.tensor_reduce(view(tile, at, [[16, 8], [1, 16]]),
                                              view(src, 0, [[256, 8], [1, 16], [16, 16]]), AX.X, ALU.add)
            else:
                ins = nc.vector.tensor_reduce(view(tile, at, [[1, 256]]), view(src, 0, [[1, 256], [256, 8]]), AX.X, ALU.add)
            step(ins)

        def apply_stat(kind, op, dst, src, stat, at):
            return TT(view(dst, 0, ALL[kind]), view(src, 0, ALL[kind]), view(stat, at, STAT[kind]), op)

        def affine(name, tile, dst):
            if name == "a":
                d = [[256, 8], [32, 8], [1, 16]]
                g, b = ([view(wrows, ROWS[k][0] + s, [[2, 8], [0, 8], [0, 16]]) for s in range(2)] for k in ("ga", "ba"))
                mul = [lambda s=s: TT(view(tile, 16 * s, d), view(tile, 16 * s, d), g[s], ALU.mult) for s in range(2)]
                add = [lambda s=s: TT(view(dst, 128 * s, [[256, 8], [16, 8], [1, 16]]), view(tile, 16 * s, d), b[s],
                                      ALU.add) for s in range(2)]
                return mul, add
            g, b = ROWS["g" + name][0], ROWS["b" + name][0]
            if name == "d":
                d, r = ALL["d"], [[0, 8], [1, 16], [0, 16]]
                add = [lambda: TT(view(dst, 0, [[16, 8], [128, 16], [1, 16]]), view(tile, 0, d), view(wrows, b, r), ALU.add)]
            else:
                d, r = ALL["e"], [[0, 64], [1, 32]]
                if name == "p":
                    add = [lambda: TT(view(dst, 0, d), view(tile, 0, d), view(wrows, b, r), ALU.add)]
                elif name == "e":
                    add = [lambda: TT(view(dst, 0, [[1, 64], [64, 32]]), view(tile, 0, d), view(wrows, b, r), ALU.add)]
                else:
                    add = [lambda i=i: TT(view(dst, 4 * i, [[16, 4], [1, 4], [64, 32]]),
                                          view(tile, 512 * i, [[128, 4], [32, 4], [1, 32]]),
                                          view(wrows, b, [[0, 4], [0, 4], [1, 32]]), ALU.add) for i in range(4)]
            return [lambda: TT(view(tile, 0, d), view(tile, 0, d), view(wrows, g, r), ALU.mult)], add

        MU = {"a": 0, "d": 512, "e": 640, "p": 704, "z": 768}
        SQ_A = 832

        def centre(name, src, dst):
            kind, at = name if name in "ade" else "e", MU[name]
            size, n = {"e": (64, 32), "d": (128, 16), "a": (256, 16)}[kind]
            if kind == "a":
                sums(mu, at + 256, src, kind)
                settle()
                for s in range(2):
                    step(TT(view(mu, at + 16 * s, HALF), view(mu, at + 256, HALF), view(mu, at + 272, HALF), ALU.add))
            else:
                sums(mu, at, src, kind)
            settle()
            step(TS(mu[:, at:at + size], mu[:, at:at + size], 1.0 / n, None, ALU.mult))
            settle()
            return apply_stat(kind, ALU.subtract, dst, src, mu, at)

        def head(t):
            dve.wait_ge(xn_ready, 2 * t + 2)
            centre("p", yt, yt).then_inc(cp_ready, 1)
            dve.wait_ge(sqp_ready, t + 1)
            sums(var, 0, sq[0], "e")
            settle()
            step(TS(var[:, 0:64], var[:, 0:64], 1.0 / 32, 1e-5, ALU.mult, ALU.add))
            settle()
            rsqrt(64, var[:, 0:64])
            step(apply_stat("e", ALU.mult, yt, yt, rs, 0))
            settle()
            mul, add = affine("p", yt, yt)
            step(mul[0]())
            settle()
            add[0]().then_inc(y_norm, 1)
            dve.wait_ge(y_norm, t + 1)
            centre("a", yt, va).then_inc(ca_ready, 1)
            dve.wait_ge(tanh_y, t + 1)
            wait(dve, sil_ready, base(t)[0])
            STT(out=sy[:, :], in0=sq[1][:, :], scalar=1.0, in1=yt[:, :], op0=ALU.add, op1=ALU.mult).then_inc(sy_ready, 1)
            centre("d", yt, vd).then_inc(cd_ready, 1)
            dve.wait_ge(sqa_ready, t + 1)
            sums(mu, SQ_A, sq[0], "a")
            settle()
            step(TT(view(var, 0, [[16, 8], [1, 16]]), view(mu, SQ_A, HALF), view(mu, SQ_A + 16, HALF), ALU.add))
            settle()
            centre("e", yt, ve).then_inc(ce_ready, 1)
            dve.wait_ge(sqd_ready, t + 1)
            sums(var, 128, sq[1], "d")
            dve.wait_ge(sqe_ready, t + 1)
            sums(var, 256, sq[0], "e")
            settle()
            step(TS(var[:, 0:256], var[:, 0:256], 1.0 / 16, 1e-5, ALU.mult, ALU.add))
            step(TS(var[:, 256:320], var[:, 256:320], 1.0 / 32, 1e-5, ALU.mult, ALU.add))
            settle()
            rsqrt(320, var[:, 0:320])
            for s in range(2):
                step(nc.vector.tensor_copy(view(rs, 384 + 16 * s, HALF), view(rs, 0, [[16, 8], [1, 16]])))
            step(apply_stat("d", ALU.mult, vd, vd, rs, 128))
            step(apply_stat("e", ALU.mult, ve, ve, rs, 256))
            settle()
            step(apply_stat("a", ALU.mult, va, va, rs, 384))
            a_mul, a_add = affine("a", va, SRC["a"])
            d_mul, d_add = affine("d", vd, SRC["d"])
            e_mul, e_add = affine("e", ve, SRC["e"])
            step(d_mul[0]())
            step(e_mul[0]())
            settle()
            for op in a_mul:
                step(op())
            settle()
            for ops in (a_add, d_add, e_add):
                for op in ops:
                    step(op())
                settle()

        def z_head(t):
            dve.wait_ge(r_loaded, 256 * t)
            TT(rbias[:, :], rscal[:, 0:1], bias_col("z"), ALU.add).then_inc(rbias_ready, 1)
            settle()
            nc.vector.memset(flag[:, 0:1], 0.0).then_inc(z_ready, 1)
            centre("z", zt, yt).then_inc(cz_ready, 1)
            dve.wait_ge(tanh_z, t)
            for i in range(4):
                STT(out=view(sz, 32 * i, [[128, 16], [1, 32]]), in0=view(sq[1], 512 * i, [[32, 16], [1, 32]]), scalar=1.0,
                    in1=view(zt, 512 * i, [[32, 16], [1, 32]]), op0=ALU.add, op1=ALU.mult).then_inc(sz_ready, 1)
            dve.wait_ge(sqz_ready, t)
            sums(var, 0, sq[0], "e")
            settle()
            step(TS(var[:, 0:64], var[:, 0:64], 1.0 / 32, 1e-5, ALU.mult, ALU.add))
            settle()
            rsqrt(64, var[:, 0:64])
            step(apply_stat("e", ALU.mult, yt, yt, rs, 0))
            settle()
            mul, add = affine("z", yt, SRC["z"])
            step(mul[0]())
            settle()
            for op in add:
                step(op())
            settle()

        def exponents(t, items, p):
            n, _, _ = counts(t, items, p)
            name, q = items[p]
            wait(dve, ext_ready, 4 * n - 4)
            for k in range(NB):
                if name in "ez":
                    v = view(SRC[name], 16 * q, [[64, 32], [1, 16]])
                    e = view(ex[q % 2], QT * k, [[16, 32], [1, 16]])
                else:
                    v = view(SRC[name], 32 * q, [[128, 16], [1, 32]])
                    e = view(ex[q % 2], QT * k, [[32, 16], [1, 32]])
                last = STT(out=e, in0=v, scalar=float(7 - 2 * k), in1=v, op0=ALU.add, op1=ALU.mult)
            last.then_inc(ex_ready, 1)

        def finish(t, items, p):
            n, m, z = counts(t, items, p)
            name, q = items[p]
            if name == "z":
                dve.wait_ge(u_ready, n + 1)
                if q == 0:
                    dve.wait_ge(res_ready, t)
                at = 512 * (q // 2) + 4 * (q % 2)
                d = [[1, 4], [1024, 2], [8, 64]]
                TT(view(res, at, d), view(res, at, d), ps_u[q % 2][:, :].rearrange("p (r a w) -> p r a w", r=4, a=2),
                   ALU.add).then_inc(o_ready, 1)
                return
            dve.wait_ge(back_ready, m + 1)
            bank = back_bank(items, p)
            if name == "a":
                for s in range(2):
                    zv = view(zt, 64 * q + 16 * s, [[256, 8], [32, 2], [1, 16]])
                    last = nc.vector.tensor_copy(zv, view(bank, s, [[2, 8], [256, 2], [16, 16]]))
            elif name == "d":
                zv = view(zt, 512 * q, [[256, 2], [16, 16], [1, 16]])
                last = TT(zv, zv, view(bank, 0, [[256, 2], [1, 16], [16, 16]]), ALU.add)
            else:
                zv = zt[:, 512 * q:512 * q + 512]
                last = TT(zv, zv, bank[:, :], ALU.add)
            last.then_inc(back_used, 1)

        def finish_last(t):
            items = quarters(t - 1)
            for p in (-2, -1):
                finish(t - 1, items, len(items) + p)
            dve.wait_ge(back_used, 12 * t)

        def body(t):
            first = isinstance(t, int) and t == 0
            head(t)
            if not first:
                finish_last(t)
                z_head(t)
            items = quarters(t)
            for p in range(len(items)):
                exponents(t, items, p)
                if p >= 2:
                    _, m, _ = counts(t, items, p - 2)
                    if items[p - 2][1] == 0 and items[p - 2][0] in "de":
                        dve.wait_ge(back_used, m)
                    finish(t, items, p - 2)

        body(0)
        head_steps = steps["n"]
        with dve.Fori(1, NT) as t:
            steps["base"] = head_steps + (t - 1) * TILE_STEPS
            steps["n"] = 0
            body(t)
            assert steps["n"] == TILE_STEPS or TILE_STEPS==0, steps["n"]
        steps["base"] = head_steps + (NT - 1) * TILE_STEPS
        steps["n"] = 0
        items = [("z", q) for q in range(4)]
        finish_last(NT)
        z_head(NT)
        for p in range(6):
            if p < 4:
                exponents(NT, items, p)
            if p >= 2:
                finish(NT, items, p - 2)

    @block.tensor
    def _(pe):
        def silu_transposed(t, items, p):
            n, _, _ = counts(t, items, p)
            name, q = items[p]
            wait(pe, silt_ready, n)
            if p == 0:
                wait(pe, back_used, base(t)[1])
            for r in range(4):
                src = SILU[name][:, 512 * q + 128 * r:512 * q + 128 * r + 128]
                last = nc.tensor.transpose(ps_sil[:, 128 * r:128 * r + 128], src, ident[:, :])
            last.then_inc(sil_ready, 1)

        def exponents_transposed(t, items, p):
            n, _, _ = counts(t, items, p)
            name, q = items[p]
            pe.wait_ge(ex_ready, n + 1)
            for g in range(4):
                wait(pe, basis_ready, 4 * n + g - 1)
                for h in range(2):
                    for r in range(4):
                        if name == "e":
                            src = view(ex[q % 2], 4 * QT * h + 4 * r + g, [[16, 128]])
                        elif name == "z":
                            src = view(ex[q % 2], 4 * QT * h + 4 * g + r, [[16, 128]])
                        else:
                            src = view(ex[q % 2], 8 * r + 2 * g + h, [[32, 128]])
                        at = 512 * h + 128 * r
                        last = nc.tensor.transpose(ps_ex[:, g % 2, at:at + 128], src, ident[:, :])
                last.then_inc(ext_ready, 1)

        def products(t, items, p):
            n, m, z = counts(t, items, p)
            name, q = items[p]
            pe.wait_ge(silt_ready, n + 1)
            if p >= 2:
                _, m_b, z_b = counts(t, items, p - 2)
                if items[p - 2][0] == "z":
                    pe.wait_ge(o_ready, z_b + 1)
                else:
                    pe.wait_ge(usb_ready, m_b + 1)
            elif not (isinstance(t, int) and t == 0):
                pe.wait_ge(usb_ready, base(t)[1] - 1 + p)
            pe.wait_ge(basis_ready, 4 * n + 4)
            u = ps_u[q % 2]
            nc.tensor.matmul(u[:, :], w_base(name), silt[q % 2][:, :], start=True, stop=False, skip_group_check=True)
            for h in range(2):
                for g in range(4):
                    at = 1024 * g + 512 * h
                    last = nc.tensor.matmul(u[32 * g:32 * g + 32, :], w_half(name, h), basis[q % 2][:, at:at + 512],
                                            start=False, stop=(h == 1), skip_group_check=True)
            last.then_inc(u_ready, 1)

        def back(t, items, p):
            n, m, _ = counts(t, items, p)
            name, q = items[p]
            if name == "z":
                return
            pe.wait_ge(usb_ready, m + 1)
            bank = back_bank(items, p)
            if bank is ps_back:
                wait(pe, back_used, m)
            for r in range(4):
                last = nc.tensor.transpose(bank[:, 128 * r:128 * r + 128], usb[q % 2][:, 128 * r:128 * r + 128],
                                           ident[:, :])
            last.then_inc(back_ready, 1)

        def body(t, tail=False):
            first = isinstance(t, int) and t == 0
            if not tail:
                pe.wait_ge(la_ready, t + 1)
                wait(pe, basis_ready, 4 * base(t)[0])
                for k in range(2):
                    for j in range(4 * k, 4 * k + 4):
                        for s in range(2):
                            at = 256 * (j - 4 * k) + 128 * s
                            last = nc.tensor.transpose(ps_ex[:, k, at:at + 128], view(la, 1024 * s + j, [[8, 128]]),
                                                       ident[:, :])
                    last.then_inc(int_ready, 1)
                pe.wait_ge(xn_ready, 2 * t + 2)
            items = quarters(t, tail)
            for p, (name, q) in enumerate(items):
                if name == "z" and q == 0:
                    pe.wait_ge(sz_ready, 4 * t)
                if name == "a" and q == 0:
                    pe.wait_ge(sy_ready, t + 1)
                    pe.wait_ge(syo_ready, 3 * t + 3)
                silu_transposed(t, items, p)
                exponents_transposed(t, items, p)
                if p >= 1:
                    products(t, items, p - 1)
                if p >= 2:
                    back(t, items, p - 2)
            n = len(items)
            products(t, items, n - 1)
            back(t, items, n - 2)
            back(t, items, n - 1)

        pe.wait_ge(w_ready, 1)
        iterations(pe, body, lambda t: body(t, True))


TILE_STEPS = 76


def pack(inputs):
    g = {k: np.asarray(v) for k, v in inputs.items()}
    f = np.float32
    cols = np.zeros((P, N_COLS), f)
    perm = np.array([2 * c + s for s in range(2) for c in range(CP)])
    for n, (name, k) in enumerate((("a", "k1"), ("d", "k2"), ("e", "k3"), ("z", "k4"))):
        ws, wb, bb = g[f"L1_conv_{k}_ws"], g[f"L1_conv_{k}_wb"], g[f"L1_conv_{k}_bb"]
        at = n * W_COLS
        if name in "ad":
            block = ws.reshape(16, 16, NB).transpose(2, 1, 0).reshape(P, 16)
            cols[:, at:at + 16] = block
            cols[:, at + 48:at + 64] = block
            for v in range(8):
                cols[16 * v:16 * v + 16, at + 64 + 16 * v:at + 80 + 16 * v] = wb.T
            cols[:, BIAS_COL + n] = np.tile(bb, 8)
        else:
            block = ws.reshape(C, C, NB)[perm][:, perm].transpose(2, 1, 0).reshape(2, P, C)
            cols[:, at:at + 32] = block[0]
            cols[:, at + 32:at + 64] = block[1]
            for v in range(4):
                cols[32 * v:32 * v + 32, at + 64 + 32 * v:at + 96 + 32 * v] = wb[perm][:, perm].T
            cols[:, BIAS_COL + n] = np.tile(bb[perm], 4)
    m = np.arange(NB) - 3.5
    cols[:, M2_COL] = np.exp(-m ** 2)[np.arange(P) // 16]
    cols[:, M2_COL + 1] = np.exp(-m ** 2)[np.arange(P) // 32]
    cols[:, M2_COL + 2] = np.exp(-m ** 2)[4 + np.arange(P) // 32]
    rows = np.zeros((1, N_ROWS), f)
    for key, value in (("gp", g["L1_conv_pn_g"][perm]), ("bp", g["L1_conv_pn_b"][perm]),
                       ("ge", g["L1_conv_k3_ln_g"][perm]), ("be", g["L1_conv_k3_ln_b"][perm]),
                       ("gz", g["L1_conv_k4_ln_g"][perm]), ("bz", g["L1_conv_k4_ln_b"][perm]),
                       ("gd", g["L1_conv_k2_ln_g"]), ("bd", g["L1_conv_k2_ln_b"]),
                       ("ga", g["L1_conv_k1_ln_g"]), ("ba", g["L1_conv_k1_ln_b"]), ("kern", g["L0_conv_kernel"].reshape(-1))):
        at, n = ROWS[key]
        rows[0, at:at + n] = value
    return cols, rows


def constants(H, W):
    nblk = -(-H // BR)
    last = H - BR * (nblk - 1)
    k = np.arange(P)
    shifts = (k[:, None, None] == np.arange(5)[None, :, None] + np.arange(BR)[None, None, :]).astype(np.float32)
    ones = np.zeros((P, nblk, W + 4), np.float32)
    ones[:BR + 4, :, 2:W + 2] = 1
    ones[:2, 0] = 0
    ones[last + 2:, nblk - 1] = 0
    mask = np.zeros((P, P), np.float32)
    mask[2:BR + 2] = 1 / (4 * H)
    return np.eye(P, dtype=np.float32), shifts, ones, mask


def kernel(**inputs):
    import concourse.bacc as bacc
    from concourse.bass_utils import run_bass_kernel_spmd

    x = np.ascontiguousarray(inputs["x"])
    cols, rows = pack(inputs)
    eye, shifts, ones, mask = constants(x.shape[2], x.shape[3])
    nc = bacc.Bacc("TRN2", target_bir_lowering=False, num_devices=1)
    arrays = {"x": x, "in_cols": cols, "in_rows": rows, "in_eye": eye, "in_shifts": shifts, "in_ones": ones, "in_mask": mask}
    args = [nc.dram_tensor(k, v.shape, mybir.dt.from_np(v.dtype), kind="ExternalInput").ap() for k, v in arrays.items()]
    out = nc.dram_tensor("result", x.shape, F32, kind="ExternalOutput").ap()
    conv_kan_kernel(nc, *args, out)
    r = run_bass_kernel_spmd(nc, [arrays], core_ids=[0])
    return r.results[0]["result"]
```

```python
import concourse.bass as bass
from concourse import mybir
from contextlib import ExitStack
import numpy as np

F32 = mybir.dt.float32
I32 = mybir.dt.int32
ALU = mybir.AluOpType
ACT = mybir.ActivationFunctionType
AX = mybir.AxisListType

P = 128
C = 32
CP = C // 2
WS = 8
NB = 8
BR = 104
FREE = WS * WS * C
QT = FREE // 4
RSQRT_GUESS = 1597463007.0

LAYERS = ("a", "d", "e", "z")
W_COLS = 192
BIAS_COL = 4 * W_COLS
M2_COL = BIAS_COL + 4
N_COLS = M2_COL + 3
ON_ACT = (0, 1, 6, 7)
ROWS = {}
_at = 0
for _n, _k in (("gp", C), ("bp", C), ("ge", C), ("be", C), ("gz", C), ("bz", C), ("gd", 16), ("bd", 16),
               ("ga", 16), ("ba", 16), ("kern", 25)):
    ROWS[_n] = (_at, _k)
    _at += _k
N_ROWS = _at


def view(tile, offset, dims, parts=P, first=0):
    step = tile[:, :].ap[0][0]
    return bass.AP(tensor=tile[:, :].tensor, offset=first * step + offset, ap=[[step, parts]] + [list(d) for d in dims])


def conv_kan_kernel(nc, x, cols, rows, ident_in, shift_in, ones_in, mask_in, centre_in, out):
    B, _, H, W = x.shape
    NG = B * CP
    NBLK = -(-H // BR)
    LAST = H - BR * (NBLK - 1)
    XW = W + 4
    NT = B * H // 16
    TB = H // 16
    CHUNKS = 2 * NBLK
    KR = BR + 4
    assert W == 512 and H % 16 == 0 and LAST % 8 == 0

    y0 = nc.dram_tensor("y0", [B, 2, CP, H, W], F32).ap()
    gn2 = nc.dram_tensor("gn2", [B, CP, 3], F32).ap()
    xg = x.rearrange("b (c s) h w -> (b c) s h w", s=2)

    ctx = ExitStack()
    with ctx:
        def sem(name):
            return ctx.enter_context(nc.semaphore(name))

        with ExitStack() as c1:
            def sb(name, shape, dt=F32):
                return c1.enter_context(nc.sbuf_tensor(name, shape, dt))

            def pb(name, n=512):
                return c1.enter_context(nc.psum_tensor(name, [P, n], F32))

            X = [sb(f"X{k}", [P, 2, NBLK, XW]) for k in range(2)]
            Y = [sb(f"Y{k}", [P, 2, NBLK, W]) for k in range(2)]
            ones = sb("ones", [P, NBLK, XW])
            shifts = sb("shifts", [P, 5, BR])
            band = sb("band", [P, 5, BR])
            gband = [sb(f"gband{k}", [P, 5, BR]) for k in range(2)]
            smap = sb("smap", [P, NBLK, W])
            kern = sb("kern", [P, 25])
            mask = sb("mask", [P, P])
            allrows = sb("allrows", [P, P])
            bs = sb("bs", [P, CHUNKS, 6])
            bsq = sb("bsq", [P, CHUNKS, 2])
            ysq = sb("ysq", [P, CHUNKS, 2])
            ys = sb("ys", [P, CHUNKS, 6])
            part1 = sb("part1", [P, 2])
            part2 = sb("part2", [P, 2 * NG])
            st = sb("st", [P, 2])
            nw = sb("nw", [P, 4])
            nrm = [sb(f"nrm{k}", [P, 1]) for k in range(2)]
            g2 = sb("g2", [P, 2 * NG])
            g2w = sb("g2w", [P, 4 * NG])
            g2o = sb("g2o", [P, NG, 3])
            pc = [pb(f"pc{k}") for k in range(NBLK)]
            pst = pb("pst")
            p2 = pb("p2")

            const_loaded = sem("const_loaded")
            cleared = sem("cleared")
            x_loaded = [sem(f"x_loaded{k}") for k in range(2)]
            y_stored = [sem(f"y_stored{k}") for k in range(2)]
            band_ready = sem("band_ready")
            part1_ready = sem("part1_ready")
            sums1_ready = sem("sums1_ready")
            gband_ready = sem("gband_ready")
            chunk_ready = sem("chunk_ready")
            chunk_used = sem("chunk_used")
            conv_done = sem("conv_done")
            y_ready = sem("y_ready")
            v1 = sem("v1")
            sums2_ready = sem("sums2_ready")
            gn2_ready = sem("gn2_ready")
            gn2_stored = sem("gn2_stored")

            block = c1.enter_context(nc.Block())
            LOADS = NBLK + 1

            @block.sync
            def _(sp):
                for dst, src in ((shifts[:, :, :], shift_in), (ones[:, :, :], ones_in), (mask[:, :], mask_in)):
                    sp.dma_start(dst, src).then_inc(const_loaded, 16)
                at, n = ROWS["kern"]
                sp.dma_start(kern[:, :], rows[:, at:at + n].partition_broadcast(P)).then_inc(const_loaded, 16)
                sp.wait_ge(cleared, 2)

                def load(k, n):
                    xn = xg[n].rearrange("s h w -> h s w")
                    sp.dma_start(X[k][2:BR + 2, :, 0, 2:W + 2], xn[0:BR]).then_inc(x_loaded[k], 16)
                    sp.dma_start(X[k][BR + 2:KR, :, 0, 2:W + 2], xn[BR:BR + 2]).then_inc(x_loaded[k], 16)
                    for b in range(1, NBLK):
                        r = KR if b < NBLK - 1 else LAST + 2
                        sp.dma_start(X[k][0:r, :, b, 2:W + 2], xn[BR * b - 2:BR * b - 2 + r]).then_inc(x_loaded[k], 16)

                load(0, 0)
                load(1, 1)
                with sp.Fori(1, NG // 2) as m:
                    for k in range(2):
                        sp.wait_ge(conv_done, 2 * m + k - 1)
                        load(k, 2 * m + k)
                sp.wait_ge(gn2_ready, 1)
                sp.dma_start(gn2.rearrange("(o b) c k -> o (b c) k", o=1), g2o[0:1, :, :]).then_inc(gn2_stored, 16)
                sp.wait_ge(gn2_stored, 16)

            @block.gpsimd
            def _(pool):
                for k in range(2):
                    nc.gpsimd.memset(X[k][:, :, :, :], 0.0).then_inc(cleared, 1)

            @block.scalar
            def _(act):
                def store(k, n):
                    yn = y0[n // CP, :, n % CP].rearrange("s h w -> h s w")
                    for b in range(NBLK):
                        r = BR if b < NBLK - 1 else LAST
                        act.dma_start(yn[BR * b:BR * b + r], Y[k][0:r, :, b, :]).then_inc(y_stored[k], 16)

                with act.Fori(0, NG // 2) as m:
                    for k in range(2):
                        act.wait_ge(y_ready, 2 * m + k + 1)
                        store(k, 2 * m + k)
                for k in range(2):
                    act.wait_ge(y_stored[k], 16 * NBLK * (NG // 2))

            @block.vector
            def _(dve):
                steps = {"base": 0, "n": 0}

                def step(ins):
                    steps["n"] += 1
                    return ins.then_inc(v1, 1)

                def settle():
                    dve.wait_ge(v1, steps["base"] + steps["n"])

                def rsqrt(y, v, h, t):
                    step(nc.vector.tensor_scalar(y.bitcast(I32), v.bitcast(I32), -0.5, RSQRT_GUESS, ALU.mult, ALU.add))
                    step(nc.vector.tensor_scalar(h, v, -0.5, None, ALU.mult))
                    for _ in range(3):
                        settle()
                        step(nc.vector.tensor_tensor(t, y, y, ALU.mult))
                        settle()
                        step(nc.vector.tensor_tensor(t, t, h, ALU.mult))
                        settle()
                        step(nc.vector.scalar_tensor_tensor(out=y, in0=t, scalar=1.5, in1=y, op0=ALU.add, op1=ALU.mult))
                    settle()

                def mean_parts(stats, sq, dst0, dst1, parts):
                    n = CHUNKS
                    means = view2(stats, 1, [[6, n], [3, 2]], parts)
                    m2 = view2(stats, 2, [[6, n], [3, 2]], parts)
                    step(nc.vector.tensor_tensor(sq[0:parts, :, :], means, means, ALU.mult))
                    settle()
                    step(nc.vector.scalar_tensor_tensor(out=sq[0:parts, :, :], in0=m2, scalar=1.0 / 256, in1=sq[0:parts, :, :],
                                                        op0=ALU.mult, op1=ALU.add))
                    settle()
                    step(nc.vector.tensor_reduce(dst0, means, AX.XY, ALU.add))
                    return nc.vector.tensor_reduce(dst1, sq[0:parts, :, :], AX.XY, ALU.add)

                def view2(tile, offset, dims, parts):
                    stp = tile[:, :, :].ap[0][0]
                    return bass.AP(tensor=tile[:, :, :].tensor, offset=offset, ap=[[stp, parts]] + dims)

                step(nc.vector.memset(allrows[:, :], 1.0 / (4 * H)))
                step(nc.vector.memset(part2[:, :], 0.0))
                step(nc.vector.memset(ys[:, :, :], 0.0))
                step(nc.vector.memset(smap[:, :, :], 0.0))
                dve.wait_ge(const_loaded, 64)
                for dy in range(5):
                    for dx in range(5):
                        w = kern[:, 5 * dy + dx:5 * dy + dx + 1]
                        if dy == 0:
                            ins = nc.vector.tensor_scalar(band[:, dx, :], shifts[:, dy, :], w, None, ALU.mult)
                        else:
                            ins = nc.vector.scalar_tensor_tensor(out=band[:, dx, :], in0=shifts[:, dy, :], scalar=w,
                                                                 in1=band[:, dx, :], op0=ALU.mult, op1=ALU.add)
                        step(ins)
                    settle()
                nc.vector.tensor_copy(kern[:, 0:1], kern[:, 0:1]).then_inc(band_ready, 1)
                for b in range(NBLK):
                    r = BR if b < NBLK - 1 else LAST
                    dve.wait_ge(chunk_ready, b + 1)
                    nc.vector.tensor_copy(smap[0:r, b, :], pc[b][0:r, :]).then_inc(chunk_used, 1)

                def sums(k, n, loads):
                    dve.wait_ge(x_loaded[k], loads)
                    for i in range(CHUNKS):
                        step(nc.vector.bn_stats(bs[0:KR, i, :], X[k][0:KR, i // NBLK, i % NBLK, 2:W + 2]))
                    settle()
                    mean_parts(bs, bsq, part1[0:KR, 0:1], part1[0:KR, 1:2], KR).then_inc(part1_ready, 1)

                def norm(k, n):
                    dve.wait_ge(sums1_ready, n + 1)
                    step(nc.vector.tensor_copy(st[:, :], pst[:, 0:2]))
                    settle()
                    step(nc.vector.tensor_tensor(nw[:, 0:1], st[:, 0:1], st[:, 0:1], ALU.mult))
                    settle()
                    step(nc.vector.tensor_tensor(nw[:, 0:1], st[:, 1:2], nw[:, 0:1], ALU.subtract))
                    settle()
                    step(nc.vector.tensor_scalar(nw[:, 0:1], nw[:, 0:1], 0.0, 1e-5, ALU.max, ALU.add))
                    settle()
                    rsqrt(nw[:, 1:2], nw[:, 0:1], nw[:, 2:3], nw[:, 3:4])
                    step(nc.vector.scalar_tensor_tensor(out=nrm[k][:, :], in0=st[:, 0:1], scalar=-1.0, in1=nw[:, 1:2],
                                                        op0=ALU.mult, op1=ALU.mult))
                    step(nc.vector.tensor_scalar(gband[k][:, :, :], band[:, :, :], nw[:, 1:2], None, ALU.mult))
                    settle()
                    nc.vector.tensor_tensor(gband[k][:, 2, :], gband[k][:, 2, :], shifts[:, 2, :],
                                            ALU.add).then_inc(gband_ready, 1)

                def evacuate(k, n, i0, i1, stored):
                    if stored is not None:
                        dve.wait_ge(y_stored[k], stored)
                    for i in range(i0, i1):
                        s, b = divmod(i, NBLK)
                        r = BR if b < NBLK - 1 else LAST
                        dve.wait_ge(chunk_ready, NBLK + CHUNKS * n + i + 1)
                        nc.vector.scalar_tensor_tensor(out=Y[k][0:r, s, b, :], in0=smap[0:r, b, :], scalar=nrm[k][0:r, 0:1],
                                                       in1=pc[i % NBLK][0:r, :], op0=ALU.mult,
                                                       op1=ALU.add).then_inc(chunk_used, 1)
                    dve.wait_ge(chunk_used, NBLK + CHUNKS * n + i1)
                    for i in range(i0, i1):
                        s, b = divmod(i, NBLK)
                        r = BR if b < NBLK - 1 else LAST
                        ins = step(nc.vector.bn_stats(ys[0:r, i, :], Y[k][0:r, s, b, :]))

                def group(k, n, stored, nxt):
                    if nxt is not None:
                        sums(1 - k, n + 1, nxt)
                    evacuate(k, n, 0, NBLK, stored)
                    if nxt is not None:
                        norm(1 - k, n + 1)
                    evacuate(k, n, NBLK, CHUNKS, None)
                    settle()
                    ins = mean_parts(ys, ysq, part2[0:BR, bass.ds(2 * n, 1)], part2[0:BR, bass.ds(2 * n + 1, 1)], BR)
                    ins.then_inc(y_ready, 1)

                PER_LOAD = 16 * LOADS
                PER_STORE = 16 * NBLK
                sums(0, 0, PER_LOAD)
                norm(0, 0)
                group(0, 0, None, PER_LOAD)
                group(1, 1, None, 2 * PER_LOAD)
                head = steps["n"]
                with dve.Fori(1, NG // 2 - 1) as m:
                    steps["n"] = 0
                    per = steps.get("per", 0)
                    steps["base"] = head + (m - 1) * GROUP_PAIR_STEPS(CHUNKS)
                    group(0, 2 * m, PER_STORE * m, PER_LOAD * (m + 1))
                    group(1, 2 * m + 1, PER_STORE * m, PER_LOAD * (m + 2))
                    assert steps["n"] == GROUP_PAIR_STEPS(CHUNKS), steps["n"]
                steps["base"] = head + (NG // 2 - 2) * GROUP_PAIR_STEPS(CHUNKS)
                steps["n"] = 0
                m = NG // 2 - 1
                group(0, 2 * m, PER_STORE * m, PER_LOAD * (m + 1))
                group(1, 2 * m + 1, PER_STORE * m, None)
                dve.wait_ge(sums2_ready, 1)
                step(nc.vector.tensor_copy(g2[:, :], p2[:, 0:2 * NG]))
                settle()
                mean, square = g2[:, 0:2 * NG:2], g2[:, 1:2 * NG:2]
                var, y, h, t = (g2w[:, q * NG:(q + 1) * NG] for q in range(4))
                step(nc.vector.tensor_tensor(var, mean, mean, ALU.mult))
                settle()
                step(nc.vector.tensor_tensor(var, square, var, ALU.subtract))
                settle()
                step(nc.vector.tensor_scalar(var, var, 0.0, 1e-5, ALU.max, ALU.add))
                settle()
                rsqrt(y, var, h, t)
                step(nc.vector.tensor_copy(g2o[:, :, 0], y))
                step(nc.vector.tensor_scalar(g2o[:, :, 2], y, 1.0, None, ALU.add))
                step(nc.vector.scalar_tensor_tensor(out=g2o[:, :, 1], in0=mean, scalar=-1.0, in1=y, op0=ALU.mult,
                                                    op1=ALU.mult))
                settle()
                nc.vector.tensor_copy(g2o[:, :, 0], y).then_inc(gn2_ready, 1)

            @block.tensor
            def _(pe):
                def conv(weights, src, bank, r):
                    for dx in range(5):
                        last = nc.tensor.matmul(pc[bank][0:BR, :], weights[0:KR, dx, :], src[0:KR, dx:dx + W],
                                                start=(dx == 0), stop=(dx == 4))
                    return last.then_inc(chunk_ready, 1)

                def sums1():
                    nc.tensor.matmul(pst[:, 0:2], mask[0:KR, :], part1[0:KR, :], start=True,
                                     stop=True).then_inc(sums1_ready, 1)

                pe.wait_ge(band_ready, 1)
                for b in range(NBLK):
                    conv(band, ones[:, b, :], b, BR)
                pe.wait_ge(part1_ready, 1)
                sums1()

                def group(k, n, more):
                    pe.wait_ge(gband_ready, n + 1)
                    for i in range(CHUNKS):
                        pe.wait_ge(chunk_used, CHUNKS * n + i + 1)
                        last = conv(gband[k], X[k][:, i // NBLK, i % NBLK, :], i % NBLK, BR)
                        if i == NBLK - 1 and more:
                            pe.wait_ge(part1_ready, n + 2)
                            sums1()
                    nc.tensor.matmul(p2[0:1, 0:1], mask[0:1, 0:1], mask[0:1, 0:1], start=True, stop=True).then_inc(conv_done, 1)

                with pe.Fori(0, NG // 2 - 1) as m:
                    group(0, 2 * m, True)
                    group(1, 2 * m + 1, True)
                group(0, NG - 2, True)
                group(1, NG - 1, False)
                pe.wait_ge(y_ready, NG)
                nc.tensor.matmul(p2[:, 0:2 * NG], allrows[0:BR, :], part2[0:BR, :], start=True,
                                 stop=True).then_inc(sums2_ready, 1)

        phase2(nc, ctx, y0, gn2, cols, rows, ident_in, centre_in, out, B, H, W, NT, TB)


def GROUP_PAIR_STEPS(chunks):
    return 2 * (chunks + 3 + 4 + 11 + 2 + chunks + 3)


def phase2(nc, ctx, y0, gn2, cols, rows, ident_in, centre_in, out, B, H, W, NT, TB):
    def sb(name, shape, dt=F32):
        return ctx.enter_context(nc.sbuf_tensor(name, shape, dt))

    def sem(name):
        return ctx.enter_context(nc.semaphore(name))

    wcols = sb("wcols", [P, N_COLS])
    wrows = sb("wrows", [P, N_ROWS])
    ident = sb("ident", [P, P])
    cmat = sb("cmat", [P, 2, 2 * P])
    la = sb("la", [P, 4 * W])
    lscal = sb("lscal", [P, 2])
    res = sb("res", [P, 4 * W])
    rscal = sb("rscal", [P, 2])
    rbias = sb("rbias", [P, 1])
    yt = sb("yt", [P, FREE])
    cb = sb("cb", [P, FREE])
    va = sb("va", [P, FREE])
    vd = sb("vd", [P, FREE])
    ve = sb("ve", [P, FREE])
    vz = sb("vz", [P, FREE])
    sy = sb("sy", [P, FREE])
    sya = sb("sya", [P, FREE])
    syd = sb("syd", [P, FREE])
    zt = sb("zt", [P, FREE])
    sz = sb("sz", [P, FREE])
    sq = sb("sq", [P, FREE])
    th = sb("th", [P, FREE])
    ex = [sb(f"ex{k}", [P, NB * QT]) for k in range(2)]
    basis = [sb(f"basis{k}", [P, 4 * 2 * 512]) for k in range(2)]
    silt = [sb(f"silt{k}", [P, 512]) for k in range(2)]
    usb = [sb(f"usb{k}", [P, 512]) for k in range(2)]
    mu = sb("mu", [P, 768])
    var = sb("var", [P, 128])
    rs = sb("rs", [P, 256])
    rsa = sb("rsa", [P, 256])
    nwh = sb("nwh", [P, 128])
    nwt = sb("nwt", [P, 128])
    flag = sb("flag", [P, 2])

    ps_sil = ctx.enter_context(nc.psum_tensor("ps_sil", [P, 512], F32))
    ps_back = ctx.enter_context(nc.psum_tensor("ps_back", [P, 512], F32))
    ps_ex = ctx.enter_context(nc.psum_tensor("ps_ex", [P, 2, 1024], F32))
    ps_u = [ctx.enter_context(nc.psum_tensor(f"ps_u{k}", [P, 512], F32)) for k in range(2)]

    w_loaded = sem("w_loaded")
    w_ready = sem("w_ready")
    l_loaded = sem("l_loaded")
    la_ready = sem("la_ready")
    int_ready = sem("int_ready")
    xn_ready = sem("xn_ready")
    ca_ready = sem("ca_ready")
    cd_ready = sem("cd_ready")
    ce_ready = sem("ce_ready")
    cz_ready = sem("cz_ready")
    sqp_ready = sem("sqp_ready")
    sqa_ready = sem("sqa_ready")
    sqd_ready = sem("sqd_ready")
    sqe_ready = sem("sqe_ready")
    sqz_ready = sem("sqz_ready")
    sq_free = sem("sq_free")
    va_ready = sem("va_ready")
    vd_ready = sem("vd_ready")
    ve_ready = sem("ve_ready")
    vz_ready = sem("vz_ready")
    y_norm = sem("y_norm")
    tanh_y = sem("tanh_y")
    sy_ready = sem("sy_ready")
    sya_ready = sem("sya_ready")
    syd_ready = sem("syd_ready")
    sye_ready = sem("sye_ready")
    z_ready = sem("z_ready")
    tanh_z = sem("tanh_z")
    sz_ready = sem("sz_ready")
    r_loaded = sem("r_loaded")
    rbias_ready = sem("rbias_ready")
    res_ready = sem("res_ready")
    ex_ready = sem("ex_ready")
    exa_ready = sem("exa_ready")
    ext_ready = sem("ext_ready")
    basis_ready = sem("basis_ready")
    sil_ready = sem("sil_ready")
    silt_ready = sem("silt_ready")
    u_ready = sem("u_ready")
    usb_ready = sem("usb_ready")
    back_ready = sem("back_ready")
    back_used = sem("back_used")
    o_ready = sem("o_ready")
    o_stored = sem("o_stored")
    v2 = sem("v2")

    WIDX = {name: n for n, name in enumerate(LAYERS)}
    SRC = {"a": va, "d": vd, "e": ve, "z": vz}
    V_READY = {"a": (va_ready, 2), "d": (vd_ready, 1), "e": (ve_ready, 1), "z": (vz_ready, 4)}
    SILU = {"a": sya, "d": syd, "e": sy, "z": sz}
    S_READY = {"a": (sya_ready, 2), "d": (syd_ready, 1), "e": (sye_ready, 1), "z": (sz_ready, 4)}
    ON_DVE = [k for k in range(NB) if k not in ON_ACT]

    def w_half(name, h):
        at = WIDX[name] * W_COLS + 32 * h
        return wcols[:, at:at + 32]

    def w_base(name):
        at = WIDX[name] * W_COLS + 64
        return wcols[:, at:at + 128]

    def bias_col(name):
        at = BIAS_COL + WIDX[name]
        return wcols[:, at:at + 1]

    def slots(t):
        names = "ade" if isinstance(t, int) and t == 0 else "z" if t is TAIL else "adze"
        return [(name, q) for name in names for q in range(4)]

    TAIL = "tail"

    class Slot:

        def __init__(self, t, p):
            items = slots(t)
            u = NT if t is TAIL else t
            zero = isinstance(u, int) and u == 0
            if p < 0:
                self.name, self.q, self.n, self.m, self.z = "e", 4 + p, 16 * u - 4 + p, 12 * u + p, None
                self.tile, self.last = u - 1, False
                return
            self.name, self.q = items[p]
            before = [name for name, _ in items[:p]]
            z = before.count("z")
            self.n = (0 if zero else 16 * u - 4) + p
            self.m = 12 * u + p - z
            self.z = 4 * u - 4 + z if not zero else None
            self.tile = u - 1 if self.name == "z" else u

    def wait(eng, s, value):
        if isinstance(value, int) and value <= 0:
            return
        eng.wait_ge(s, value)

    def iterations(eng, start, body, tail, before=None):
        start()
        body(0, True)
        with eng.Fori(1, NT - 1) as t:
            if before is not None:
                before(t)
            body(t, True)
            if before is not None:
                before(None)
        if before is not None:
            before(NT - 1)
        body(NT - 1, False)
        tail()

    def bias_m(k):
        return float(3.5 - k)

    def operands(w, k):
        if w.name in "ez":
            return view(SRC[w.name], 16 * w.q, [[64, 32], [1, 16]]), view(ex[w.q % 2], QT * k, [[16, 32], [1, 16]])
        return view(SRC[w.name], 32 * w.q, [[128, 16], [1, 32]]), view(ex[w.q % 2], QT * k, [[32, 16], [1, 32]])

    def uses(name, u):
        if isinstance(u, int) and u == 0:
            return {"a": 4, "d": 8, "e": 12}[name]
        return 16 * u + {"a": 0, "d": 4, "e": 12}[name]

    def squares(k, u):
        return k + 1 if isinstance(u, int) and u == 0 else 5 * u + k

    def squares_z(t):
        return 5 * NT if isinstance(t, int) and t == NT else 5 * t + 4

    def tiles(t):
        return NT if isinstance(t, int) and t == NT else t + 1

    block = ctx.enter_context(nc.Block())

    @block.sync
    def _(sp):
        sp.dma_start(wcols[:, :], cols).then_inc(w_loaded, 16)
        sp.dma_start(wrows[:, :], rows.partition_broadcast(P)).then_inc(w_loaded, 16)
        sp.dma_start(ident[:, :], ident_in).then_inc(w_loaded, 16)
        sp.dma_start(cmat[:, :, :], centre_in).then_inc(w_loaded, 16)

        def load_windows(t):
            b, r0 = t // TB, (t % TB) * 16
            wait(sp, int_ready, 4 * t)
            for s in range(2):
                for wr in range(2):
                    src = y0[b, s, :, bass.ds(r0 + 8 * wr, 8), :]
                    at = 1024 * s + 512 * wr
                    sp.dma_start(la[:, at:at + 512], src).then_inc(l_loaded, 16)
            sp.dma_start(lscal[:, :], gn2[b, :, 0:2].unsqueeze(1).to_broadcast([CP, WS, 2])).then_inc(l_loaded, 16)

        def load_result(t):
            b, r0 = t // TB, (t % TB) * 16
            for g in range(4):
                for s in range(2):
                    src = y0[b, s, :, bass.ds(r0, 16), :].rearrange("c (wr g i) w -> g c wr (i w)", wr=2, i=2)[g]
                    p0 = 32 * g + 16 * s
                    sp.dma_start(res[p0:p0 + 16, :].rearrange("p (r w) -> p r w", r=2), src).then_inc(r_loaded, 16)
                    sp.dma_start(rscal[p0:p0 + 16, :], gn2[b, :, 1:3]).then_inc(r_loaded, 16)

        def store_result(t):
            b, r0 = t // TB, (t % TB) * 16
            sp.wait_ge(o_ready, 4 * t + 4)
            ov = out[b].rearrange("(c s) h w -> s c h w", s=2)
            for g in range(4):
                for s in range(2):
                    dst = ov[s, :, bass.ds(r0, 16), :].rearrange("c (wr g i) w -> g c wr (i w)", wr=2, i=2)[g]
                    p0 = 32 * g + 16 * s
                    sp.dma_start(dst, res[p0:p0 + 16, :].rearrange("p (r w) -> p r w", r=2)).then_inc(o_stored, 16)

        load_windows(0)
        load_windows(1)
        load_result(0)
        with sp.Fori(1, NT - 1) as t:
            load_windows(t + 1)
            store_result(t - 1)
            sp.wait_ge(o_stored, 128 * t)
            load_result(t)
        store_result(NT - 2)
        sp.wait_ge(o_stored, 128 * (NT - 1))
        load_result(NT - 1)
        store_result(NT - 1)
        sp.wait_ge(o_stored, 128 * NT)

    @block.scalar
    def _(act):
        A = nc.scalar.activation

        def normalise_rows(u):
            act.wait_ge(l_loaded, 80 * (u + 1))
            A(la[:, :], la[:, :], ACT.Identity, scale=lscal[:, 0:1], bias=lscal[:, 1:2]).then_inc(la_ready, 1)

        def windows(u, k):
            act.wait_ge(int_ready, 4 * u + k + 1)
            if k == 0:
                wait(act, ce_ready, u)
            A(view(yt, 64 * k, [[1, 64], [256, 8]]), ps_sil[:, :].rearrange("p (f i) -> p f i", i=8),
              ACT.Copy).then_inc(xn_ready, 1)

        def square(src, dst_ready, src_ready, count, free):
            act.wait_ge(src_ready, count)
            wait(act, sq_free, free)
            A(sq[:, :], src[:, :], ACT.Square).then_inc(dst_ready, 1)

        def square_p(u):
            square(yt, sqp_ready, xn_ready, 4 * u + 4, squares(0, u) - 1)

        def square_a(u):
            square(cb, sqa_ready, ca_ready, u + 1, squares(1, u) - 1)

        def square_d(u):
            square(cb, sqd_ready, cd_ready, u + 1, squares(2, u) - 1)

        def square_e(u):
            square(cb, sqe_ready, ce_ready, u + 1, squares(3, u) - 1)

        def square_z(t):
            square(cb, sqz_ready, cz_ready, t, squares_z(t) - 1)

        def tanh_of_y(u):
            act.wait_ge(y_norm, u + 1)
            wait(act, sz_ready, 4 * (u - 1))
            wait(act, sye_ready, u)
            A(th[:, :], yt[:, :], ACT.Tanh, scale=0.5).then_inc(tanh_y, 1)

        def tanh_of_z(t):
            act.wait_ge(z_ready, t)
            act.wait_ge(sye_ready, tiles(t))
            A(th[:, :], zt[:, :], ACT.Tanh, scale=0.5).then_inc(tanh_z, 1)

        def silu_a(u):
            act.wait_ge(sy_ready, u + 1)
            if not (isinstance(u, int) and u == 0):
                act.wait_ge(sil_ready, uses("a", u - 1))
            for s in range(2):
                A(view(sya, s, [[2, 8], [256, 8], [16, 16]]), view(th, 16 * s, [[256, 8], [32, 8], [1, 16]]),
                  ACT.Copy).then_inc(sya_ready, 1)

        def silu_d(u):
            if not (isinstance(u, int) and u == 0):
                act.wait_ge(sil_ready, uses("d", u - 1))
            A(view(syd, 0, [[256, 8], [1, 16], [16, 16]]), view(th, 0, [[256, 8], [16, 16], [1, 16]]),
              ACT.Copy).then_inc(syd_ready, 1)

        def silu_e(u):
            if not (isinstance(u, int) and u == 0):
                act.wait_ge(sil_ready, uses("e", u - 1))
            A(sy[:, :], th[:, :], ACT.Copy).then_inc(sye_ready, 1)

        def residual(t):
            act.wait_ge(rbias_ready, t)
            A(res[:, :], res[:, :], ACT.Identity, scale=rscal[:, 1:2], bias=rbias[:, 0:1]).then_inc(res_ready, 1)

        def exponent(w, i):
            k = ON_ACT[i]
            if i == 0:
                ready, per = V_READY[w.name]
                act.wait_ge(ready, per * (w.tile + 1))
                wait(act, ext_ready, 4 * w.n - 4)
            v, e = operands(w, k)
            ins = A(e, v, ACT.Square, bias=bias_m(k))
            if i == len(ON_ACT) - 1:
                ins.then_inc(exa_ready, 1)

        def evacuate(w):
            if w.name == "z":
                return
            act.wait_ge(u_ready, w.n + 1)
            wait(act, back_ready, w.m - 1)
            A(usb[w.q % 2][:, :], ps_u[w.q % 2][:, :], ACT.Identity, bias=bias_col(w.name)).then_inc(usb_ready, 1)

        def slot(t, p, ahead):
            w = Slot(t, p)
            act.wait_ge(sil_ready, w.n + 1)
            wait(act, u_ready, w.n - 1)
            A(silt[w.q % 2][:, :], ps_sil[:, :], ACT.Copy).then_inc(silt_ready, 1)
            for g in range(4):
                act.wait_ge(ext_ready, 4 * w.n + g + 1)
                A(basis[w.q % 2][:, 1024 * g:1024 * g + 1024], ps_ex[:, g % 2, :], ACT.Exp,
                  scale=-1.0).then_inc(basis_ready, 1)
                if ahead is not None:
                    for i in range(len(ON_ACT) * g // 4, len(ON_ACT) * (g + 1) // 4):
                        exponent(ahead, i)

        def start():
            act.wait_ge(w_ready, 1)
            normalise_rows(0)
            for k in range(4):
                windows(0, k)
            square_p(0)
            tanh_of_y(0)
            square_a(0)
            silu_a(0)
            silu_d(0)
            square_d(0)
            square_e(0)
            for i in range(len(ON_ACT)):
                exponent(Slot(0, 0), i)

        def body(t, more):
            first = isinstance(t, int) and t == 0
            if more:
                normalise_rows(t + 1)
            n = len(slots(t))
            for p in range(n):
                slot(t, p, Slot(t, p + 1) if p + 1 < n else Slot(t + 1, 0) if more else None)
                pieces(t, p, more)
                if not (first and p == 0):
                    evacuate(Slot(t, p - 1))

        def pieces(t, p, more):
            first = isinstance(t, int) and t == 0
            u, at = t + 1, ACT_SLOTS[first]
            if p == 0:
                silu_e(t)
            if more and p < 4:
                windows(u, p)
            if not first:
                if p == 2:
                    tanh_of_z(t)
                if p == 3:
                    square_z(t)
                if p == 4:
                    residual(t)
            if more:
                if p == at["p"]:
                    square_p(u)
                if p == at["tanh"]:
                    tanh_of_y(u)
                if p == at["a"]:
                    square_a(u)
                if p == at["sa"]:
                    silu_a(u)
                if p == at["sd"]:
                    silu_d(u)
                if p == at["d"]:
                    square_d(u)
                if p == at["e"]:
                    square_e(u)

        def tail():
            evacuate(Slot(TAIL, -1))
            tanh_of_z(NT)
            square_z(NT)
            residual(NT)
            for i in range(len(ON_ACT)):
                exponent(Slot(TAIL, 0), i)
            for p in range(4):
                slot(TAIL, p, Slot(TAIL, p + 1) if p < 3 else None)

        iterations(act, start, body, tail)

    @block.vector
    def _(dve):
        steps = {"base": 0, "n": 0}

        def step(ins):
            steps["n"] += 1
            return ins.then_inc(v2, 1)

        def settle():
            dve.wait_ge(v2, steps["base"] + steps["n"])

        TT, TS, STT = nc.vector.tensor_tensor, nc.vector.tensor_scalar, nc.vector.scalar_tensor_tensor

        dve.wait_ge(w_loaded, 64)
        at, end = ROWS["ge"][0], ROWS["kern"][0]
        step(TS(wrows[:, at:end], wrows[:, at:end], 1.75, None, ALU.mult))
        for name in LAYERS:
            step(TS(w_base(name), w_base(name), 0.5, None, ALU.mult))
            for h in range(2):
                col = M2_COL + (0 if name in "ad" else 1 + h)
                step(TS(w_half(name, h), w_half(name, h), wcols[:, col:col + 1], None, ALU.mult))
        settle()
        nc.vector.memset(flag[:, :], 0.0).then_inc(w_ready, 1)

        ALL = {"e": [[32, 64], [1, 32]], "d": [[256, 8], [16, 16], [1, 16]], "a": [[256, 8], [1, 256]]}
        STAT = {"e": [[1, 64], [0, 32]], "d": [[16, 8], [0, 16], [1, 16]], "a": [[0, 8], [1, 256]]}
        HALF = [[32, 8], [1, 16]]
        MU = {"a": 0, "d": 512, "e": 640, "z": 704}

        def sums(tile, at, src, kind):
            if kind == "e":
                ins = nc.vector.tensor_reduce(view(tile, at, [[1, 64]]), view(src, 0, [[32, 64], [1, 32]]), AX.X, ALU.add)
            elif kind == "d":
                ins = nc.vector.tensor_reduce(view(tile, at, [[16, 8], [1, 16]]),
                                              view(src, 0, [[256, 8], [1, 16], [16, 16]]), AX.X, ALU.add)
            else:
                ins = nc.vector.tensor_reduce(view(tile, at, [[1, 256]]), view(src, 0, [[1, 256], [256, 8]]), AX.X, ALU.add)
            return ins

        def apply_stat(kind, op, dst, src, stat, at):
            return TT(view(dst, 0, ALL[kind]), view(src, 0, ALL[kind]), view(stat, at, STAT[kind]), op)

        def centre(name, src, dst):
            kind, at = name if name in "ade" else "e", MU[name]
            size, n = {"e": (64, 32), "d": (128, 16), "a": (256, 16)}[kind]
            if kind == "a":
                step(sums(mu, at + 256, src, kind))
                settle()
                for s in range(2):
                    step(TT(view(mu, at + 16 * s, HALF), view(mu, at + 256, HALF), view(mu, at + 272, HALF), ALU.add))
            else:
                step(sums(mu, at, src, kind))
            settle()
            step(TS(mu[:, at:at + size], mu[:, at:at + size], 1.0 / n, None, ALU.mult))
            settle()
            return apply_stat(kind, ALU.subtract, dst, src, mu, at)

        def divide(name, tile):
            kind = name if name in "ade" else "e"
            n, size = {"e": (64, 32), "d": (128, 16), "a": (128, 16)}[kind]
            if kind == "a":
                sums(mu, MU["a"] + 256, sq, "a").then_inc(sq_free, 1)
                settle_on(sq_free)
                step(TT(view(var, 0, [[16, 8], [1, 16]]), view(mu, MU["a"] + 256, HALF), view(mu, MU["a"] + 272, HALF),
                        ALU.add))
            else:
                sums(var, 0, sq, kind).then_inc(sq_free, 1)
                settle_on(sq_free)
            settle()
            v = var[:, 0:n]
            step(TS(v, v, 1.0 / size, 1e-5, ALU.mult, ALU.add))
            settle()
            y, h, t = rs[:, 0:n], nwh[:, 0:n], nwt[:, 0:n]
            step(TS(y.bitcast(I32), v.bitcast(I32), -0.5, RSQRT_GUESS, ALU.mult, ALU.add))
            step(TS(h, v, -0.5, None, ALU.mult))
            for _ in range(3):
                settle()
                step(TT(t, y, y, ALU.mult))
                settle()
                step(TT(t, t, h, ALU.mult))
                settle()
                step(STT(out=y, in0=t, scalar=1.5, in1=y, op0=ALU.add, op1=ALU.mult))
            settle()
            stat = rs
            if kind == "a":
                for s in range(2):
                    step(nc.vector.tensor_copy(view(rsa, 16 * s, HALF), view(rs, 0, [[16, 8], [1, 16]])))
                settle()
                stat = rsa
            step(apply_stat(kind, ALU.mult, tile, tile, stat, 0))

        freed = {"count": 0}

        def settle_on(_):
            dve.wait_ge(sq_free, freed["count"])

        def affine(name, tile, dst, ready):
            settle()
            if name == "a":
                d = [[256, 8], [32, 8], [1, 16]]
                g, b = ([view(wrows, ROWS[k][0] + s, [[2, 8], [0, 8], [0, 16]]) for s in range(2)] for k in ("ga", "ba"))
                for s in range(2):
                    step(TT(view(tile, 16 * s, d), view(tile, 16 * s, d), g[s], ALU.mult))
                settle()
                for s in range(2):
                    TT(view(dst, 128 * s, [[256, 8], [16, 8], [1, 16]]), view(tile, 16 * s, d), b[s],
                       ALU.add).then_inc(ready, 1)
                return
            g, b = ROWS["g" + name][0], ROWS["b" + name][0]
            d, r = (ALL["d"], [[0, 8], [1, 16], [0, 16]]) if name == "d" else (ALL["e"], [[0, 64], [1, 32]])
            step(TT(view(tile, 0, d), view(tile, 0, d), view(wrows, g, r), ALU.mult))
            settle()
            if name == "z":
                for i in range(4):
                    TT(view(dst, 4 * i, [[16, 4], [1, 4], [64, 32]]), view(tile, 512 * i, [[128, 4], [32, 4], [1, 32]]),
                       view(wrows, b, [[0, 4], [0, 4], [1, 32]]), ALU.add).then_inc(ready, 1)
                return
            o = {"d": [[16, 8], [128, 16], [1, 16]], "p": d, "e": [[1, 64], [64, 32]]}[name]
            TT(view(dst, 0, o), view(tile, 0, d), view(wrows, b, r), ALU.add).then_inc(ready, 1)

        def divide_p(u):
            dve.wait_ge(sqp_ready, u + 1)
            freed["count"] = squares(0, u)
            divide("p", yt)

        def affine_p(u):
            affine("p", yt, yt, y_norm)

        def centre_a(u):
            dve.wait_ge(y_norm, u + 1)
            centre("a", yt, cb).then_inc(ca_ready, 1)

        def silu_y(u):
            dve.wait_ge(tanh_y, u + 1)
            STT(out=th[:, :], in0=th[:, :], scalar=1.0, in1=yt[:, :], op0=ALU.add, op1=ALU.mult).then_inc(sy_ready, 1)

        def divide_a(u):
            dve.wait_ge(sqa_ready, u + 1)
            freed["count"] = squares(1, u)
            divide("a", cb)

        def affine_a(u):
            if not (isinstance(u, int) and u == 0):
                dve.wait_ge(exa_ready, uses("a", u - 1))
                dve.wait_ge(ex_ready, uses("a", u - 1))
            affine("a", cb, va, va_ready)

        def centre_d(u):
            dve.wait_ge(va_ready, 2 * u + 2)
            centre("d", yt, cb).then_inc(cd_ready, 1)

        def divide_d(u):
            dve.wait_ge(sqd_ready, u + 1)
            freed["count"] = squares(2, u)
            divide("d", cb)

        def affine_d(u):
            if not (isinstance(u, int) and u == 0):
                dve.wait_ge(exa_ready, uses("d", u - 1))
                dve.wait_ge(ex_ready, uses("d", u - 1))
            affine("d", cb, vd, vd_ready)

        def centre_e(u):
            dve.wait_ge(vd_ready, u + 1)
            centre("e", yt, cb).then_inc(ce_ready, 1)

        def divide_e(u):
            dve.wait_ge(sqe_ready, u + 1)
            freed["count"] = squares(3, u)
            divide("e", cb)

        def affine_e(u):
            if not (isinstance(u, int) and u == 0):
                dve.wait_ge(exa_ready, uses("e", u - 1))
                dve.wait_ge(ex_ready, uses("e", u - 1))
            affine("e", cb, ve, ve_ready)

        def start_z(t):
            dve.wait_ge(back_used, 12 * t)
            dve.wait_ge(r_loaded, 256 * t)
            TT(rbias[:, :], rscal[:, 0:1], bias_col("z"), ALU.add).then_inc(rbias_ready, 1)
            nc.vector.memset(flag[:, 0:1], 0.0).then_inc(z_ready, 1)
            dve.wait_ge(ve_ready, tiles(t))
            centre("z", zt, cb).then_inc(cz_ready, 1)

        def silu_z(t):
            dve.wait_ge(tanh_z, t)
            dve.wait_ge(sil_ready, 16 * t - 8)
            for i in range(4):
                STT(out=view(sz, 32 * i, [[128, 16], [1, 32]]), in0=view(th, 512 * i, [[32, 16], [1, 32]]), scalar=1.0,
                    in1=view(zt, 512 * i, [[32, 16], [1, 32]]), op0=ALU.add, op1=ALU.mult).then_inc(sz_ready, 1)
            dve.wait_ge(sz_ready, 4 * t)

        def divide_z(t):
            dve.wait_ge(sqz_ready, t)
            freed["count"] = squares_z(t)
            divide("z", cb)

        def affine_z(t):
            dve.wait_ge(exa_ready, 16 * t - 8)
            dve.wait_ge(ex_ready, 16 * t - 8)
            affine("z", cb, vz, vz_ready)

        def exponents(w):
            ready, per = V_READY[w.name]
            dve.wait_ge(ready, per * (w.tile + 1))
            wait(dve, ext_ready, 4 * w.n - 4)
            for k in ON_DVE:
                v, e = operands(w, k)
                last = STT(out=e, in0=v, scalar=float(7 - 2 * k), in1=v, op0=ALU.add, op1=ALU.mult)
            last.then_inc(ex_ready, 1)

        def finish(w):
            q = w.q
            if w.name == "z":
                dve.wait_ge(u_ready, w.n + 1)
                if q == 0:
                    dve.wait_ge(res_ready, w.tile + 1)
                at = 512 * (q // 2) + 4 * (q % 2)
                d = [[1, 4], [1024, 2], [8, 64]]
                TT(view(res, at, d), view(res, at, d), ps_u[q % 2][:, :].rearrange("p (r a w) -> p r a w", r=4, a=2),
                   ALU.add).then_inc(o_ready, 1)
                return
            dve.wait_ge(back_ready, w.m + 1)
            if q == 0 and w.name in "de":
                dve.wait_ge(back_used, w.m)
            if w.name == "a":
                for s in range(2):
                    zv = view(zt, 64 * q + 16 * s, [[256, 8], [32, 2], [1, 16]])
                    last = nc.vector.tensor_copy(zv, view(ps_back, s, [[2, 8], [256, 2], [16, 16]]))
            elif w.name == "d":
                zv = view(zt, 512 * q, [[256, 2], [16, 16], [1, 16]])
                last = TT(zv, zv, view(ps_back, 0, [[256, 2], [1, 16], [16, 16]]), ALU.add)
            else:
                zv = zt[:, 512 * q:512 * q + 512]
                last = TT(zv, zv, ps_back[:, :], ALU.add)
            last.then_inc(back_used, 1)

        def start():
            divide_p(0)
            affine_p(0)
            centre_a(0)
            silu_y(0)
            divide_a(0)
            affine_a(0)
            centre_d(0)
            divide_d(0)
            affine_d(0)
            centre_e(0)
            exponents(Slot(0, 0))

        def body(t, more):
            first = isinstance(t, int) and t == 0
            n = len(slots(t))
            for p in range(n):
                if p + 1 < n:
                    exponents(Slot(t, p + 1))
                elif more:
                    exponents(Slot(t + 1, 0))
                if not first and p == 3:
                    silu_z(t)
                if not first or p >= 3:
                    w = Slot(t, p - 3)
                    if w.name != "z":
                        finish(w)
                if p >= 2:
                    w = Slot(t, p - 2)
                    if w.name == "z":
                        finish(w)
                pieces(t, p, more)

        def pieces(t, p, more):
            first = isinstance(t, int) and t == 0
            u, at = t + 1, DVE_SLOTS[first]
            if p == 0:
                divide_e(t)
            if p == 1:
                affine_e(t)
            if not first:
                if p == 2:
                    start_z(t)
                if p == 4:
                    divide_z(t)
                if p == 5:
                    affine_z(t)
            if more:
                if p == at["p1"]:
                    divide_p(u)
                if p == at["p2"]:
                    affine_p(u)
                if p == at["ca"]:
                    centre_a(u)
                if p == at["sy"]:
                    silu_y(u)
                if p == at["a1"]:
                    divide_a(u)
                if p == at["a2"]:
                    affine_a(u)
                if p == at["cd"]:
                    centre_d(u)
                if p == at["d1"]:
                    divide_d(u)
                if p == at["d2"]:
                    affine_d(u)
                if p == at["ce"]:
                    centre_e(u)

        def tail():
            for p in (-3, -2, -1):
                finish(Slot(TAIL, p))
            start_z(NT)
            silu_z(NT)
            divide_z(NT)
            affine_z(NT)
            exponents(Slot(TAIL, 0))
            for p in range(4):
                if p < 3:
                    exponents(Slot(TAIL, p + 1))
                if p >= 2:
                    finish(Slot(TAIL, p - 2))
            finish(Slot(TAIL, 2))
            finish(Slot(TAIL, 3))

        start_steps = {}

        def before(t):
            if t is None:
                assert steps["n"] == TILE_STEPS, steps["n"]
                return
            start_steps.setdefault("n", steps["n"])
            steps["base"] = start_steps["n"] + (t - 1) * TILE_STEPS
            steps["n"] = 0

        iterations(dve, start, body, tail, before)

    @block.tensor
    def _(pe):
        def windows(u, k):
            if k == 0:
                pe.wait_ge(la_ready, u + 1)
            wait(pe, xn_ready, 4 * u + k)
            for jl in range(2):
                for s in range(2):
                    last = nc.tensor.matmul(ps_sil[:, 256 * jl:256 * jl + 256], view(la, 1024 * s + 2 * k + jl, [[8, 128]]),
                                            cmat[:, s, :], start=(s == 0), stop=(s == 1))
            last.then_inc(int_ready, 1)

        def silu_transposed(w):
            ready, per = S_READY[w.name]
            pe.wait_ge(ready, per * (w.tile + 1))
            wait(pe, silt_ready, w.n)
            for r in range(4):
                src = SILU[w.name][:, 512 * w.q + 128 * r:512 * w.q + 128 * r + 128]
                last = nc.tensor.transpose(ps_sil[:, 128 * r:128 * r + 128], src, ident[:, :])
            last.then_inc(sil_ready, 1)

        def exponents_transposed(w):
            pe.wait_ge(ex_ready, w.n + 1)
            pe.wait_ge(exa_ready, w.n + 1)
            for g in range(4):
                wait(pe, basis_ready, 4 * w.n + g - 1)
                for h in range(2):
                    for r in range(4):
                        if w.name == "e":
                            src = view(ex[w.q % 2], 4 * QT * h + 4 * r + g, [[16, 128]])
                        elif w.name == "z":
                            src = view(ex[w.q % 2], 4 * QT * h + 4 * g + r, [[16, 128]])
                        else:
                            src = view(ex[w.q % 2], 8 * r + 2 * g + h, [[32, 128]])
                        at = 512 * h + 128 * r
                        last = nc.tensor.transpose(ps_ex[:, g % 2, at:at + 128], src, ident[:, :])
                last.then_inc(ext_ready, 1)

        def products(w, before):
            pe.wait_ge(silt_ready, w.n + 1)
            if before is not None:
                if before.name == "z":
                    pe.wait_ge(o_ready, before.z + 1)
                else:
                    pe.wait_ge(usb_ready, before.m + 1)
            pe.wait_ge(basis_ready, 4 * w.n + 4)
            u = ps_u[w.q % 2]
            nc.tensor.matmul(u[:, :], w_base(w.name), silt[w.q % 2][:, :], start=True, stop=False, skip_group_check=True)
            for h in range(2):
                for g in range(4):
                    at = 1024 * g + 512 * h
                    last = nc.tensor.matmul(u[32 * g:32 * g + 32, :], w_half(w.name, h), basis[w.q % 2][:, at:at + 512],
                                            start=False, stop=(h == 1), skip_group_check=True)
            last.then_inc(u_ready, 1)

        def back(w):
            if w.name == "z":
                return
            pe.wait_ge(usb_ready, w.m + 1)
            wait(pe, back_used, w.m)
            for r in range(4):
                last = nc.tensor.transpose(ps_back[:, 128 * r:128 * r + 128], usb[w.q % 2][:, 128 * r:128 * r + 128],
                                           ident[:, :])
            last.then_inc(back_ready, 1)

        def start():
            pe.wait_ge(w_ready, 1)
            for k in range(4):
                windows(0, k)

        def body(t, more):
            first = isinstance(t, int) and t == 0
            for p in range(len(slots(t))):
                w = Slot(t, p)
                if more and p in (1, 2, 3, 4) or p == 0:
                    wait(pe, xn_ready, 4 * t + 4 + p)
                silu_transposed(w)
                exponents_transposed(w)
                if more and p < 4:
                    wait(pe, silt_ready, w.n + 1)
                    windows(t + 1, p)
                if not first or p >= 1:
                    products(Slot(t, p - 1), Slot(t, p - 3) if not first or p >= 3 else None)
                if not first or p >= 2:
                    back(Slot(t, p - 2))

        def tail():
            products(Slot(TAIL, -1), Slot(TAIL, -3))
            back(Slot(TAIL, -2))
            back(Slot(TAIL, -1))
            for p in range(4):
                silu_transposed(Slot(TAIL, p))
                exponents_transposed(Slot(TAIL, p))
                if p >= 1:
                    products(Slot(TAIL, p - 1), Slot(TAIL, p - 3))
            products(Slot(TAIL, 3), Slot(TAIL, 1))

        iterations(pe, start, body, tail)


ACT_SLOTS = {True: {"p": 3, "tanh": 6, "a": 6, "sa": 8, "sd": 9, "d": 9, "e": 11},
             False: {"p": 5, "tanh": 8, "a": 8, "sa": 10, "sd": 11, "d": 12, "e": 15}}
DVE_SLOTS = {True: {"p1": 4, "p2": 5, "ca": 6, "sy": 7, "a1": 7, "a2": 8, "cd": 8, "d1": 10, "d2": 11, "ce": 11},
             False: {"p1": 6, "p2": 7, "ca": 8, "sy": 9, "a1": 9, "a2": 10, "cd": 11, "d1": 13, "d2": 14, "ce": 14}}
TILE_STEPS = 84


def pack(inputs):
    g = {k: np.asarray(v) for k, v in inputs.items()}
    f = np.float32
    cols = np.zeros((P, N_COLS), f)
    perm = np.array([2 * c + s for s in range(2) for c in range(CP)])
    for n, (name, k) in enumerate((("a", "k1"), ("d", "k2"), ("e", "k3"), ("z", "k4"))):
        ws, wb, bb = g[f"L1_conv_{k}_ws"], g[f"L1_conv_{k}_wb"], g[f"L1_conv_{k}_bb"]
        at = n * W_COLS
        if name in "ad":
            block = ws.reshape(16, 16, NB).transpose(2, 1, 0).reshape(P, 16)
            cols[:, at:at + 16] = block
            cols[:, at + 48:at + 64] = block
            for v in range(8):
                cols[16 * v:16 * v + 16, at + 64 + 16 * v:at + 80 + 16 * v] = wb.T
            cols[:, BIAS_COL + n] = np.tile(bb, 8)
        else:
            block = ws.reshape(C, C, NB)[perm][:, perm].transpose(2, 1, 0).reshape(2, P, C)
            cols[:, at:at + 32] = block[0]
            cols[:, at + 32:at + 64] = block[1]
            for v in range(4):
                cols[32 * v:32 * v + 32, at + 64 + 32 * v:at + 96 + 32 * v] = wb[perm][:, perm].T
            cols[:, BIAS_COL + n] = np.tile(bb[perm], 4)
    m = np.arange(NB) - 3.5
    factor = np.where(np.isin(np.arange(NB), ON_ACT), 1.0, np.exp(-m ** 2))
    cols[:, M2_COL] = factor[np.arange(P) // 16]
    cols[:, M2_COL + 1] = factor[np.arange(P) // 32]
    cols[:, M2_COL + 2] = factor[4 + np.arange(P) // 32]
    rows = np.zeros((1, N_ROWS), f)
    for key, value in (("gp", g["L1_conv_pn_g"][perm]), ("bp", g["L1_conv_pn_b"][perm]),
                       ("ge", g["L1_conv_k3_ln_g"][perm]), ("be", g["L1_conv_k3_ln_b"][perm]),
                       ("gz", g["L1_conv_k4_ln_g"][perm]), ("bz", g["L1_conv_k4_ln_b"][perm]),
                       ("gd", g["L1_conv_k2_ln_g"]), ("bd", g["L1_conv_k2_ln_b"]),
                       ("ga", g["L1_conv_k1_ln_g"]), ("ba", g["L1_conv_k1_ln_b"]), ("kern", g["L0_conv_kernel"].reshape(-1))):
        at, n = ROWS[key]
        rows[0, at:at + n] = value
    return cols, rows


def constants(H, W):
    nblk = -(-H // BR)
    last = H - BR * (nblk - 1)
    k = np.arange(P)
    shifts = (k[:, None, None] == np.arange(5)[None, :, None] + np.arange(BR)[None, None, :]).astype(np.float32)
    ones = np.zeros((P, nblk, W + 4), np.float32)
    ones[:BR + 4, :, 2:W + 2] = 1
    ones[:2, 0] = 0
    ones[last + 2:, nblk - 1] = 0
    mask = np.zeros((P, P), np.float32)
    mask[2:BR + 2] = 1 / (4 * H)
    col = np.arange(2 * P)
    centre = np.zeros((P, 2, 2 * P), np.float32)
    for s in range(2):
        centre[:, s] = (k[:, None] + P * s == col[None, :]) - (k[:, None] % WS == col[None, :] % WS) / C
    return np.eye(P, dtype=np.float32), shifts, ones, mask, centre


def kernel(**inputs):
    import concourse.bacc as bacc
    from concourse.bass_utils import run_bass_kernel_spmd

    x = np.ascontiguousarray(inputs["x"])
    cols, rows = pack(inputs)
    eye, shifts, ones, mask, centre = constants(x.shape[2], x.shape[3])
    nc = bacc.Bacc("TRN2", target_bir_lowering=False, num_devices=1)
    arrays = {"x": x, "in_cols": cols, "in_rows": rows, "in_eye": eye, "in_shifts": shifts, "in_ones": ones, "in_mask": mask, "in_centre": centre}
    args = [nc.dram_tensor(k, v.shape, mybir.dt.from_np(v.dtype), kind="ExternalInput").ap() for k, v in arrays.items()]
    out = nc.dram_tensor("result", x.shape, F32, kind="ExternalOutput").ap()
    conv_kan_kernel(nc, *args, out)
    r = run_bass_kernel_spmd(nc, [arrays], core_ids=[0])
    return r.results[0]["result"]
```
